# Optimizing a Trainium2 kernel written in Bass

```python
import numpy as np
import jax
import jax.numpy as jnp

def _softmax(x, axis=-1):
    return jax.nn.softmax(x, axis=axis)
def _gelu(x):
    return jax.nn.gelu(x, approximate=True)
def _silu(x):
    return jax.nn.silu(x)
def _sigmoid(x):
    return jax.nn.sigmoid(x)
def _layernorm(x, axis=-1, eps=1e-5):
    m = jnp.mean(x, axis=axis, keepdims=True)
    v = jnp.var(x, axis=axis, keepdims=True)
    return (x - m) / jnp.sqrt(v + eps)
def _scatter_add(tgt, idx, src, axis=0):
    return tgt.at[idx].add(src)
def _segment_sum(src, seg, n):
    return jax.ops.segment_sum(src, seg, n)

kernel_name = 'mk_conv_preact_d1_conv_nchw512_4d1f68'

def setup_inputs(seed: int = 0):
    np.random.seed(seed)
    _w = jnp.asarray
    def _rec_inputs():
        import jax
        import jax.numpy as jnp
        _gk = jax.random.key(seed)
        x = 7.22e-05 + 1 * jax.random.normal(jax.random.fold_in(_gk, 1), (16, 512, 32, 32), jnp.float32)
        return x
    x = _rec_inputs()
    def _L0_conv_setup():
        import jax, jax.numpy as jnp
        import numpy as np
        NUM_HEADS = 8
        HEAD_SIZE = 64
        N_EMBED = 512
        key = jax.random.key(seed)
        ks = jax.random.split(key, 6)
        B, C, H, W = (16, N_EMBED, 32, 32)
        x = jax.random.normal(ks[0], (B, C, H, W), dtype=jnp.float32)
        s = 1.0 / np.sqrt(N_EMBED)
        Wq = jax.random.normal(ks[1], (NUM_HEADS, N_EMBED, HEAD_SIZE), dtype=jnp.float32) * s
        Wk = jax.random.normal(ks[2], (NUM_HEADS, N_EMBED, HEAD_SIZE), dtype=jnp.float32) * s
        Wv = jax.random.normal(ks[3], (NUM_HEADS, N_EMBED, HEAD_SIZE), dtype=jnp.float32) * s
        Wproj = jax.random.normal(ks[4], (NUM_HEADS * HEAD_SIZE, N_EMBED), dtype=jnp.float32) * s
        bproj = jax.random.normal(ks[5], (N_EMBED,), dtype=jnp.float32) * 0.01
        return {'x': x, 'Wq': Wq, 'Wk': Wk, 'Wv': Wv, 'Wproj': Wproj, 'bproj': bproj}
    _L0_conv_all = _L0_conv_setup()
    _L0_conv_in = {k: v for k, v in _L0_conv_all.items() if k in ('Wq', 'Wk', 'Wv', 'Wproj', 'bproj', )}
    del _L0_conv_all

    return {
        "x": x,
        "L0_conv_Wq": _L0_conv_in["Wq"],
        "L0_conv_Wk": _L0_conv_in["Wk"],
        "L0_conv_Wv": _L0_conv_in["Wv"],
        "L0_conv_Wproj": _L0_conv_in["Wproj"],
        "L0_conv_bproj": _L0_conv_in["bproj"],
    }

def reference(x, L0_conv_Wq, L0_conv_Wk, L0_conv_Wv, L0_conv_Wproj, L0_conv_bproj):
    import jax
    import jax.numpy as jnp
    def _L0_conv_ref(x, Wq, Wk, Wv, Wproj, bproj):
        import jax, jax.numpy as jnp
        import numpy as np
        NUM_HEADS = 8
        HEAD_SIZE = 64
        N_EMBED = 512
        B, C, H, W = x.shape
        T = H * W
        xs = jnp.reshape(x, (B, T, C))
        q = jnp.einsum('btc,hcd->bhtd', xs, Wq)
        k = jnp.einsum('btc,hcd->bhtd', xs, Wk)
        v = jnp.einsum('btc,hcd->bhtd', xs, Wv)
        scale = 1.0 / jnp.sqrt(jnp.asarray(HEAD_SIZE, dtype=x.dtype))
        scores = jnp.einsum('bhtd,bhsd->bhts', q, k) * scale
        att = jax.nn.softmax(scores, axis=-1)
        out = jnp.einsum('bhts,bhsd->bhtd', att, v)
        out = jnp.transpose(out, (0, 2, 1, 3)).reshape(B, T, -1)
        out = out @ Wproj + bproj
        return jnp.reshape(out, (B, C, H, W))

    def _gn(v, G=32, eps=1e-5):
        B_, C_, H_, W_ = v.shape
        g = v.reshape(B_, G, C_ // G, H_, W_)
        m = jnp.mean(g, axis=(2, 3, 4), keepdims=True)
        s = jnp.var(g, axis=(2, 3, 4), keepdims=True)
        return ((g - m) / jnp.sqrt(s + eps)).reshape(v.shape)

    def _ln_c(v, eps=1e-6):
        m = jnp.mean(v, axis=1, keepdims=True)
        s = jnp.var(v, axis=1, keepdims=True)
        return (v - m) / jnp.sqrt(s + eps)

    def _ln_t(v, eps=1e-5):
        m = jnp.mean(v, axis=-1, keepdims=True)
        s = jnp.var(v, axis=-1, keepdims=True)
        return (v - m) / jnp.sqrt(s + eps)

    def _to_tokens(v):
        B_, C_, H_, W_ = v.shape
        return v.reshape(B_, C_, H_ * W_).transpose(0, 2, 1)
    def _from_tokens(t, like):
        B_, C_, H_, W_ = like.shape
        return t.transpose(0, 2, 1).reshape(B_, C_, H_, W_)

    x = x + _L0_conv_ref(_gn(x), L0_conv_Wq, L0_conv_Wk, L0_conv_Wv, L0_conv_Wproj, L0_conv_bproj)
    return x


_drawn_inputs = setup_inputs


def setup_inputs(seed=0):
    import zlib

    import numpy as np

    out = dict(_drawn_inputs(seed))
    spreads = {}
    factors = {'L0_conv_bproj': 5.544}
    for name, (base, spread) in spreads.items():
        noise = np.random.default_rng([zlib.crc32(name.encode()), seed]).standard_normal(out[name].shape)
        drawn = base * np.exp(spread * noise) if base else spread * noise
        out[name] = jnp.asarray(drawn.astype(out[name].dtype))
    for name, factor in factors.items():
        out[name] = (out[name] * factor).astype(out[name].dtype)
    return out
```

```python
from contextlib import ExitStack

import concourse.bass as bass
from concourse import mybir

F32 = mybir.dt.float32
F32R = mybir.dt.float32r
ALU = mybir.AluOpType
ACT = mybir.ActivationFunctionType
AX = mybir.AxisListType

P = 128
GROUPS = 32
EPS = 1e-5
ST, SM, PVB, WB = 0, 2, 4, 6

CHUNKS = {"qk": 4, "v": 4, "xt": 4, "proj": 4, "mean": 1, "var": 1, "mt": 1}
RES = 3
BLOCKS = 16
AHEAD = 2
POOL_BLOCKS = (1, 5, 7, 9, 11, 13, 15)


def fillers(h, has_next):
    slots = [[] for _ in range(BLOCKS)]
    slots[0] += [("mt", 1, 0, 1)]
    if h < 7:
        slots[0] += [("qk", 0, 0, 4)]
        if h == 6:
            slots[1] += [("qk", 1, 0, 4)]
        else:
            slots[1] += [("qk", 1, 0, 2)]
            slots[2] += [("qk", 1, 2, 4)]
    elif has_next:
        slots[0] += [("xt", 5, 0, 4)]
        slots[1] += [("xt", 6, 0, 4)]
        slots[2] += [("xt", 7, 0, 4), ("qk", 0, 0, 4)]
        slots[3] += [("qk", 1, 0, 4)]
        for e, s in enumerate((4, 8, 11, 13)):
            slots[s] += [("v", e, 0, 4)]
    if h in (1, 2):
        slots[4] += [("v", 4 + 2 * (h - 1), 0, 4)]
        slots[9] += [("v", 5 + 2 * (h - 1), 0, 4)]
    if h == 3 and has_next:
        slots[6] += [("mean", 0, 0, 1)]
        slots[8] += [("var", 0, 0, 1)]
    if h == 6 and has_next:
        for t in range(4):
            slots[2 + t] += [("xt", t, 0, 4)]
        slots[10] += [("mean", 1, 0, 1)]
        slots[12] += [("var", 1, 0, 1)]
        slots[14] += [("xt", 4, 0, 4)]
    if not (h == 7 and not has_next):
        slots[11] += [("mt", 0, 0, 1)]
    return slots


PROJ_SLOTS = (3, 4, 5, 6, 8, 10, 12, 14)


def max_blocks(h, has_next):
    if h == 7 and not has_next:
        return [0] * BLOCKS
    return [0] * 6 + [2, 1, 2, 2, 2, 2, 2, 1, 2, 0]


class Plan:

    def __init__(self, batches):
        self.prologue = [("mean", 0), ("var", 0)] + [("xt", t) for t in range(4)]
        self.prologue += [("mean", 1), ("var", 1)] + [("xt", t) for t in range(4, 8)]
        self.prologue += [("qk", 0), ("qk", 1), ("v", 0), ("v", 1), ("mt", 0), ("v", 2), ("v", 3)]
        self.place = {("start", 0, e): n for n, e in enumerate(self.prologue)}
        n = len(self.prologue)
        self.steps = {}
        for section, ks in (("first", [0]), ("body", range(1, 9)), ("last", range(1, 8))):
            if section == "last":
                n = body_start + self.per_batch * (batches - 1)
            if section == "body":
                body_start = n
            for k in ks:
                has_next = section != "last"
                slots = fillers(k % 8, has_next)
                if section == "body" and k == 8:
                    for t, s in enumerate(PROJ_SLOTS):
                        slots[s] = slots[s] + [("proj", t, 0, 4)]
                assert not slots[BLOCKS - 1]
                opened = []
                for s, slot in enumerate(slots):
                    for kind, a, lo, hi in slot:
                        if lo == 0:
                            opened.append(s)
                        assert len(opened) < 3 or opened[-3] < s
                self.steps[section, k] = slots
                for s in slots:
                    for kind, a, lo, hi in s:
                        if lo == 0:
                            self.place[section, k, (kind, a)] = n
                            n += 1
            if section == "body":
                self.per_batch = n - body_start
        for t in range(8):
            self.place["last", 8, ("proj", t)] = n + t
        assert self.per_batch % 2 == 0


class Step:

    def __init__(self, eng, it, section, k, plan, last_batch, bases):
        self.eng, self.it, self.section, self.k = eng, it, section, k
        self.plan, self.bases = plan, bases
        self.h = k % 8
        self.has_next = section != "last"
        self.slots = plan.steps.get((section, k))
        self.looped = section == "body"

    def at(self, per_batch, const):
        if not self.looped:
            return per_batch * self.it + const
        if per_batch not in self.bases:
            self.bases[per_batch] = self.eng.snap(self.it * per_batch)
        return self.bases[per_batch] + const

    def heads(self, per_head, ahead=0, more=0):
        return self.at(8 * per_head, per_head * (self.k + ahead) + more)

    def batches(self, per_batch, more):
        return self.at(per_batch, more)

    def bank(self, kind, arg, back=0):
        n = self.plan.place[self.section, self.k - back, (kind, arg)]
        per = self.plan.per_batch
        if self.looped:
            return n % 2, self.at(per // 2, n // 2)
        return n % 2, n // 2

    def done(self, slot):
        pieces = self.slots[slot - 1] if slot else []
        return [(kind, a) for kind, a, lo, hi in pieces if hi == CHUNKS[kind]]


def attention_block(nc, x, Wq, Wk, Wv, Wproj, bproj, out):
    B, C, H_, W_ = x.shape
    T = H_ * W_
    NH, _, D = Wq.shape
    CH = C // P
    TT = T // P
    TC = T // 512
    SCALE = D ** -0.5
    PER_GROUP = T // GROUPS
    assert (C, T, NH, D, CH, TT, TC) == (512, 1024, 8, 64, 4, 8, 2)
    plan = Plan(B)

    xv = x.rearrange("b c h w -> b (c h w)").rearrange("b (k p c) -> b p k c", p=P, c=C)
    ov = out.rearrange("b c h w -> b (c h w)").rearrange("b (k p c) -> b p k c", p=P, c=C)
    inv_dram = nc.dram_tensor("inv_dram", (1, 512), F32).ap()

    with ExitStack() as ctx:
        def sb(name, shape, dt=F32):
            return ctx.enter_context(nc.sbuf_tensor(name, shape, dt))

        def sem(name):
            return ctx.enter_context(nc.semaphore(name))

        wqk_h = sb("wqk_h", [P, CH, NH, P], F32R)
        wqk_l = sb("wqk_l", [P, CH, NH, P], F32R)
        wv_h = sb("wv_h", [P, CH, C], F32R)
        wv_l = sb("wv_l", [P, CH, C], F32R)
        wp = sb("wp", [P, CH, C])
        bias = sb("bias", [P, C])
        ident = sb("ident", [P, P])
        group_avg = sb("group_avg", [P, P])
        xh = sb("xh", [P, CH, T], F32R)
        xl = sb("xl", [P, CH, T], F32R)
        VW = 2 * D + 1
        vh = sb("vh", [P, TT, NH // 2, VW], F32R)
        vl = sb("vl", [P, TT, NH // 2, VW], F32R)
        q_hh = sb("q_hh", [P, 2, T], F32R)
        q_lm = sb("q_lm", [P, 2, T], F32R)
        k_hl = sb("k_hl", [P, 2, T], F32R)
        k_h1 = sb("k_h1", [P, 2, T], F32R)
        prob = sb("prob", [P, 2, 512])
        prob_h = sb("prob_h", [P, 3, 512], F32R)
        prob_l = sb("prob_l", [P, 3, 512], F32R)
        acc = sb("acc", [P, 512])
        inv_b = sb("inv_b", [P, 512])
        den = sb("den", [32, 16])
        inv = sb("inv", [32, 16])
        o = sb("o", [P, NH // 2, T])
        xs = sb("xs", [P, 4, C])
        res = sb("res", [P, RES, C])
        smax = sb("smax", [P, 2 * BLOCKS])
        nmax = sb("nmax", [P, TT])
        mrow = sb("mrow", [4, 2, P], F32R)
        bn = sb("bn", [P, 4, 6])
        mv = sb("mv", [P, 4, 2])
        gmean = sb("gmean", [P, 4])
        dev = sb("dev", [P, 4])
        dev2 = sb("dev2", [P, 4])
        spread = sb("spread", [P, 4])
        gvar = sb("gvar", [P, 4])
        rstd = sb("rstd", [P, 4])
        minus_half = sb("minus_half", [P, 4])

        ps = [ctx.enter_context(nc.psum_tensor(f"bank{n}", [P, 512], F32)) for n in range(8)]

        weights_in = sem("weights_in")
        wv_in = sem("wv_in")
        wp_in = sem("wp_in")
        bias_in = sem("bias_in")
        x_in = sem("x_in")
        res_in = [sem(f"res_in{n}") for n in range(RES)]
        y_out = [sem(f"y_out{n}") for n in range(RES)]
        den_in = sem("den_in")
        inv_out = sem("inv_out")
        inv_in = sem("inv_in")
        mrow_in = [sem("mrow_in0"), sem("mrow_in1")]
        w_hi = sem("w_hi")
        w_lo = sem("w_lo")
        consts = sem("consts")
        v_cols = sem("v_cols")
        stat_done = sem("stat_done")
        rstd_ready = sem("rstd_ready")
        xn_ready = sem("xn_ready")
        mean_done = sem("mean_done")
        var_done = sem("var_done")
        xt_done = sem("xt_done")
        qk_done = sem("qk_done")
        v_done = sem("v_done")
        mt_done = sem("mt_done")
        proj_done = sem("proj_done")
        xt_hi = sem("xt_hi")
        qk_hi = sem("qk_hi")
        qk_twice = [sem("qk_twice0"), sem("qk_twice1")]
        v_hi = sem("v_hi")
        taken = [sem("taken0"), sem("taken1")]
        scores_ready = sem("scores_ready")
        rows_ready = sem("rows_ready")
        rows_used = sem("rows_used")
        nmax_ready = sem("nmax_ready")
        prob_ready = sem("prob_ready")
        prob_h_ready = sem("prob_h_ready")
        prob_l_ready = sem("prob_l_ready")
        prob_l_pool = sem("prob_l_pool")
        pv_done = sem("pv_done")
        acc_ready = sem("acc_ready")
        inv_ready = sem("inv_ready")
        o_ready = sem("o_ready")
        res_bias = sem("res_bias")

        per_pool = len(POOL_BLOCKS)
        per_dve = BLOCKS - per_pool

        def lo_wait(eng, s, i):
            ahead, i = divmod(i, BLOCKS)
            if i in POOL_BLOCKS:
                eng.wait_ge(prob_l_pool, s.heads(per_pool, ahead, POOL_BLOCKS.index(i) + 1))
            else:
                n = sum(j not in POOL_BLOCKS for j in range(i + 1))
                eng.wait_ge(prob_l_ready, s.heads(per_dve, ahead, n))

        def entry_taken(eng, s, kind, a, back=0):
            bank, before = s.bank(kind, a, back)
            eng.wait_ge(taken[bank], before + 1)

        def start_taken(eng, kind, a):
            n = plan.place["start", 0, (kind, a)]
            eng.wait_ge(taken[n % 2], n // 2 + 1)

        def tile_count(s, t, credit=16):
            r = t % RES
            return s.batches(16 * len(range(r, TT, RES)), credit + 16 * (t // RES + 1))

        def rows(h):
            return (slice(0, D), D) if h % 2 == 0 else (slice(D, P), D - 1)

        def run(eng, step):
            step(Step(eng, 0, "first", 0, plan, B, None))
            with eng.Fori(0, B - 1) as it:
                bases = {}
                for k in range(1, 9):
                    step(Step(eng, it, "body", k, plan, B, bases))
            for k in range(1, 8):
                step(Step(eng, B - 1, "last", k, plan, B, None))

        def ring3(s, i):
            return (BLOCKS * s.h + i) % (BLOCKS * NH) % 3

        block = ctx.enter_context(nc.Block())

        @block.sync
        def _(sp):
            raw_qk = o[:, :, :].rearrange("p a t -> p (a t)").rearrange("p (c h m) -> p c h m", c=CH, h=NH)
            sp.dma_start(xs[:, :, :], xv[0, :, 0:4, :]).then_inc(x_in, 16)
            for r in range(RES):
                sp.sem_inc(y_out[r], 16)
            for c in range(CH):
                for half, w in ((0, Wq), (1, Wk)):
                    sp.dma_start(raw_qk[:, c, :, half * D:(half + 1) * D],
                                 w[:, c * P:(c + 1) * P, :].rearrange("h p d -> p h d")).then_inc(weights_in, 16)
                sp.dma_start(wp[:, c, :].rearrange("p (h d) -> p h d", h=NH),
                             Wv[:, c * P:(c + 1) * P, :].rearrange("h p d -> p h d")).then_inc(wv_in, 16)
            sp.dma_start(bias[:, :], bproj.partition_broadcast(P)).then_inc(bias_in, 16)
            sp.wait_ge(xt_done, 4)
            sp.dma_start(xs[:, :, :], xv[0, :, 4:8, :]).then_inc(x_in, 16)
            sp.wait_ge(w_lo, 2)
            sp.dma_start(wp[:, :, :], Wproj.rearrange("(c p) n -> p c n", p=P)).then_inc(wp_in, 16)

            def max_row(half, slot):
                sp.dma_start(q_lm[D:D + 1, slot, half * 512:(half + 1) * 512].bitcast(F32),
                             mrow[:, half, :].bitcast(F32)).then_inc(mrow_in[half], 16)

            def twice(a, slot, count):
                sp.wait_ge(qk_hi, count)
                cols = slice(a * 512, (a + 1) * 512)
                sp.dma_start(q_hh[D:P, slot, cols].bitcast(F32),
                             q_hh[0:D, slot, cols].bitcast(F32)).then_inc(qk_twice[a], 16)
                sp.dma_start(k_hl[0:D, slot, cols].bitcast(F32),
                             k_h1[0:D, slot, cols].bitcast(F32)).then_inc(qk_twice[a], 16)

            twice(0, 0, 1)
            twice(1, 0, 2)
            start_taken(sp, "mt", 0)
            max_row(0, 0)

            def den_to_square(s, ahead, tc):
                sp.wait_ge(acc_ready, s.heads(2, ahead, tc + 1))
                r = rows(s.h + ahead)[1]
                sp.dma_start(den[:, :], acc[r:r + 1, :]).then_inc(den_in, 16)

            def inv_to_rows(s, ahead, tc):
                sp.wait_ge(inv_ready, s.heads(2, ahead, tc + 1))
                sp.dma_start(inv_dram[0:1, :].rearrange("a (p f) -> (a p) f", p=32), inv[:, :]).then_inc(inv_out, 16)
                sp.wait_ge(inv_out, s.heads(32, ahead, 16 * (tc + 1)))
                sp.dma_start(inv_b[rows(s.h + ahead)[0], :],
                             inv_dram[0, :].partition_broadcast(D)).then_inc(inv_in, 16)

            def residual(s, t, b):
                sp.wait_ge(y_out[t % RES], tile_count(s, t - RES))
                sp.dma_start(res[:, t % RES, :], xv[b, :, t, :]).then_inc(res_in[t % RES], 16)

            def store(s, t, b):
                entry_taken(sp, s, "proj", t)
                sp.dma_start(ov[b, :, t, :], res[:, t % RES, :]).then_inc(y_out[t % RES], 16)

            def step(s):
                first = s.section == "first"
                for i in range(BLOCKS):
                    if i == 1:
                        entry_taken(sp, s, "mt", 1)
                        max_row(1, s.k % 2)
                    if i == 1 and not first:
                        den_to_square(s, -1, 1)
                    for kind, a in s.done(i):
                        if kind == "qk":
                            twice(a, (s.k + 1) % 2, s.heads(2, 1, a + 1))
                    if i == 4 and not first:
                        inv_to_rows(s, -1, 1)
                    if i == 9:
                        den_to_square(s, 0, 0)
                    if i == 12:
                        if not (s.h == 7 and not s.has_next):
                            entry_taken(sp, s, "mt", 0)
                            max_row(0, (s.k + 1) % 2)
                        inv_to_rows(s, 0, 0)
                    if s.h == 2 and i == 8 and s.has_next:
                        sp.wait_ge(xt_done, s.batches(8, 8))
                        sp.dma_start(xs[:, :, :], xv[s.it + 1, :, 0:4, :]).then_inc(x_in, 16)
                    if s.h == 6 and i == 6 and s.has_next:
                        sp.wait_ge(xt_done, s.batches(8, 12))
                        sp.dma_start(xs[:, :, :], xv[s.it + 1, :, 4:8, :]).then_inc(x_in, 16)
                    if s.section == "body" and s.k == 8:
                        if i < RES:
                            residual(s, i, s.it)
                        for t, at in enumerate(PROJ_SLOTS):
                            if i == at + 1:
                                store(s, t, s.it)
                                if 1 <= t <= TT - RES:
                                    residual(s, t + RES - 1, s.it)

            run(sp, step)
            s = Step(sp, B - 1, "last", 8, plan, B, None)
            den_to_square(s, -1, 1)
            for t in range(RES):
                residual(s, t, B - 1)
            inv_to_rows(s, -1, 1)
            for t in range(TT):
                store(s, t, B - 1)
                if 1 <= t <= TT - RES:
                    residual(s, t + RES - 1, B - 1)
            for t in range(TT - RES, TT):
                sp.wait_ge(y_out[t % RES], tile_count(s, t))

        @block.tensor
        def _(pe):
            def split_product(bank, cols, pairs, start, stop):
                n = len(pairs)
                for j, (w, m) in enumerate(pairs):
                    last = nc.tensor.matmul(ps[bank][:, cols], w, m, start=start and j == 0,
                                            stop=stop and j == n - 1)
                return last

            def entry(kind, a, lo, hi, bank, before, s_h, s_slot, wait):
                w = ps[WB + bank]
                if lo == 0 and before is not None:
                    pe.wait_ge(taken[bank], before)
                wait()
                if kind == "qk":
                    cols = slice(a * 512, (a + 1) * 512)
                    for c in range(lo, hi):
                        last = split_product(WB + bank, slice(0, 512),
                                             [(wqk_h[:, c, s_h, :], xh[:, c, cols]),
                                              (wqk_l[:, c, s_h, :], xh[:, c, cols]),
                                              (wqk_h[:, c, s_h, :], xl[:, c, cols])], c == 0, c == CH - 1)
                    if hi == CH:
                        last.then_inc(qk_done, 1)
                elif kind == "v":
                    half, e = divmod(a, 4)
                    vcols = slice(half * 256, (half + 1) * 256)
                    for j in range(2):
                        t = slice((2 * e + j) * P, (2 * e + j + 1) * P)
                        for c in range(CH):
                            last = split_product(WB + bank, slice(j * 256, (j + 1) * 256),
                                                 [(xh[:, c, t], wv_h[:, c, vcols]),
                                                  (xh[:, c, t], wv_l[:, c, vcols]),
                                                  (xl[:, c, t], wv_h[:, c, vcols])], c == 0, c == CH - 1)
                    last.then_inc(v_done, 1)
                elif kind == "xt":
                    for c in range(CH):
                        last = nc.tensor.transpose(w[:, c * P:(c + 1) * P], xs[:, a % 4, c * P:(c + 1) * P],
                                                   ident[:, :])
                    last.then_inc(xt_done, 1)
                elif kind == "mean":
                    nc.tensor.matmul(w[:, 0:4], group_avg[:, :], mv[:, :, 0], start=True, stop=True).then_inc(mean_done, 1)
                elif kind == "var":
                    nc.tensor.matmul(w[:, 0:4], group_avg[:, :], spread[:, :], start=True, stop=True).then_inc(var_done, 1)
                elif kind == "mt":
                    nc.tensor.matmul(w[0:4, 0:P], nmax[:, a * 4:(a + 1) * 4], ident[:, :],
                                     start=True, stop=True).then_inc(mt_done, 1)
                elif kind == "proj":
                    for c in range(CH):
                        last = nc.tensor.matmul(w[:, :], o[:, c, a * P:(a + 1) * P], wp[:, c, :],
                                                start=c == 0, stop=c == CH - 1)
                    last.then_inc(proj_done, 1)

            def scores(slot, i, n_bank, wait):
                tc, t = divmod(i, TT)
                keys, queries = slice(t * P, (t + 1) * P), slice(tc * 512, (tc + 1) * 512)
                wait()
                s_bank = ps[ST + n_bank]
                nc.tensor.matmul(s_bank[:, :], k_hl[:, slot, keys], q_hh[:, slot, queries], start=True, stop=False)
                nc.tensor.matmul(s_bank[:, :], k_h1[0:D + 1, slot, keys], q_lm[0:D + 1, slot, queries],
                                 start=False, stop=True).then_inc(scores_ready, 1)

            def row_scores(slot, j):
                t, half = divmod(j, 2)
                nc.tensor.matmul(ps[SM + j % 2][:, :], q_hh[:, slot, t * P:(t + 1) * P],
                                 k_hl[:, slot, half * 512:(half + 1) * 512], start=True, stop=True).then_inc(rows_ready, 1)

            nothing = lambda: None
            n = 0

            def start_entry(kind, a, h=0, wait=nothing):
                pos = plan.place["start", 0, (kind, a)]
                before = pos // 2 if pos >= 2 else None
                entry(kind, a, 0, 4 if kind in ("qk", "v", "xt") else 1, pos % 2, before, h, 0, wait)

            pe.wait_ge(consts, 9)
            for half in range(2):
                start_entry("mean", half, wait=lambda: pe.wait_ge(stat_done, 11 * half + 8))
                start_entry("var", half, wait=lambda: start_taken(pe, "mean", half))
                for t in range(4 * half, 4 * half + 4):
                    start_entry("xt", t, wait=lambda: pe.wait_ge(xn_ready, t + 1))
            pe.wait_ge(w_hi, 2)
            pe.wait_ge(w_lo, 2)
            for tc in range(2):
                for t in range(4 * tc + 2, 4 * tc + 4):
                    start_taken(pe, "xt", t)
                start_entry("qk", tc)
            start_entry("v", 0)
            start_entry("v", 1)
            for tc in range(2):
                start_taken(pe, "qk", tc)
                pe.wait_ge(qk_twice[tc], 32)
            for j in range(BLOCKS):
                if j >= 2:
                    pe.wait_ge(rows_used, j - 1)
                row_scores(0, j)
                if j == 9:
                    start_entry("mt", 0, wait=lambda: pe.wait_ge(nmax_ready, 1))
            start_entry("v", 2)
            start_entry("v", 3)
            scores(0, 0, 0, lambda: pe.wait_ge(mrow_in[0], 16))
            scores(0, 1, 1, nothing)
            pe.wait_ge(v_cols, 2)
            pe.wait_ge(wp_in, 16)

            def step(s):
                first = s.section == "first"
                end = s.h == 7 and not s.has_next
                hi_j = 0
                per_slot = max_blocks(s.h, s.has_next)
                for i in range(BLOCKS):
                    ahead, j = divmod(i + AHEAD, BLOCKS)
                    if not (end and ahead):
                        def wait():
                            pe.wait_ge(prob_h_ready, s.heads(BLOCKS, 0, i + 1))
                            if j == 0:
                                pe.wait_ge(mrow_in[0], s.heads(16, 1, 16))
                            if j == TT:
                                pe.wait_ge(mrow_in[1], s.heads(16, 0, 16))
                        scores((s.k + ahead) % 2, j, j % 2, wait)
                    tc, t = divmod(i, TT)
                    pair = s.h // 2
                    if t == 0 and not first:
                        pe.wait_ge(acc_ready, s.heads(2, -1, tc + 1))
                    if tc == 0 and t % 2 == 0 and s.h in (0, 4):
                        if first:
                            start_taken(pe, "v", t // 2)
                        elif s.h == 0:
                            entry_taken(pe, s, "v", t // 2, back=1)
                        else:
                            entry_taken(pe, s, "v", 4 + t // 2, back=3 - t // 4)
                    lo_wait(pe, s, i)
                    ring = ring3(s, i)
                    c0 = 0 if s.h % 2 == 0 else 1
                    v_hi_op, v_lo_op = vh[:, t, pair, c0:c0 + P], vl[:, t, pair, c0:c0 + P]
                    bank = PVB + tc
                    nc.tensor.matmul(ps[bank][:, :], v_hi_op, prob_h[:, ring, :], start=t == 0, stop=False)
                    nc.tensor.matmul(ps[bank][:, :], v_lo_op, prob_h[:, ring, :], start=False, stop=False)
                    nc.tensor.matmul(ps[bank][:, :], v_hi_op, prob_l[:, ring, :],
                                     start=False, stop=t == TT - 1).then_inc(pv_done, 1)
                    for kind, a, lo, hi in s.slots[i]:
                        bk, before = s.bank(kind, a)

                        def wait():
                            if kind == "xt":
                                pe.wait_ge(xn_ready, s.batches(8, 8 + a + 1))
                            if kind == "mean":
                                pe.wait_ge(stat_done, s.batches(22, 22 + 11 * a + 8))
                            if kind == "var":
                                entry_taken(pe, s, "mean", a)
                            if kind == "mt":
                                pe.wait_ge(nmax_ready, s.heads(2, 0 if a else 1, 2 if a else 1))
                            if kind == "proj" and a in (0, 4):
                                pe.wait_ge(o_ready, s.heads(2, 0, -1 if a == 0 else 0))
                        entry(kind, a, lo, hi, bk, before, (s.h + 1) % NH, 0, wait)
                    for _ in range(per_slot[i]):
                        if hi_j == 0:
                            if s.bank("qk", 0)[0] != s.bank("qk", 1)[0]:
                                entry_taken(pe, s, "qk", 0)
                            entry_taken(pe, s, "qk", 1)
                            for a in range(2):
                                pe.wait_ge(qk_twice[a], s.heads(32, 1, 32))
                        pe.wait_ge(rows_used, s.heads(BLOCKS, 1, hi_j - 1))
                        row_scores((s.k + 1) % 2, hi_j)
                        hi_j += 1

            run(pe, step)
            s = Step(pe, B - 1, "last", 8, plan, B, None)
            pe.wait_ge(o_ready, 2 * NH * B)
            for t in range(TT):
                bk, before = s.bank("proj", t)
                entry("proj", t, 0, 4, bk, before, 0, 0, nothing)

        @block.scalar
        def _(act):
            raw_qk = o[:, :, :].rearrange("p a t -> p (a t)").rearrange("p (c h m) -> p c h m", c=CH, h=NH)

            def exp_block(ring2, ring3, bank, wait_p, wait_h):
                wait_p()
                nc.scalar.activation(prob[:, ring2, :], ps[ST + bank][:, :], ACT.Exp, scale=SCALE).then_inc(prob_ready, 1)
                wait_h()
                nc.scalar.activation(prob_h[:, ring3, :], ps[ST + bank][:, :], ACT.Exp, scale=SCALE).then_inc(prob_h_ready, 1)

            def take(kind, a, bank, slot, h, count):
                w = ps[WB + bank]
                if kind == "xt":
                    act.wait_ge(xt_done, count)
                    nc.scalar.copy(xh[:, :, a * P:(a + 1) * P],
                                   w[:, :].rearrange("p (c t) -> p c t", c=CH)).then_inc(xt_hi, 1)
                if kind == "qk":
                    cols = slice(a * 512, (a + 1) * 512)
                    act.wait_ge(qk_done, count)
                    nc.scalar.copy(q_hh[0:D, slot, cols], w[0:D, :])
                    nc.scalar.copy(k_h1[0:D, slot, cols], w[D:P, :]).then_inc(qk_hi, 1)
                if kind == "v":
                    half, e = divmod(a, 4)
                    act.wait_ge(v_done, count)
                    for j in range(2):
                        for odd in range(2):
                            last = nc.scalar.copy(
                                vh[:, 2 * e + j, 2 * half:2 * half + 2, odd * (D + 1):odd * (D + 1) + D],
                                w[:, j * 256:(j + 1) * 256].rearrange("p (a o d) -> p o a d", o=2, d=D)[:, odd])
                    last.then_inc(v_hi, 1)

            act.wait_ge(weights_in, 128)
            nc.scalar.copy(wqk_h[:, :, :, :], raw_qk).then_inc(w_hi, 1)
            act.wait_ge(wv_in, 64)
            nc.scalar.copy(wv_h[:, :, :], wp[:, :, :]).then_inc(w_hi, 1)
            act.wait_ge(v_cols, 2)
            for kind, a in plan.prologue:
                if kind in ("xt", "qk", "v"):
                    take(kind, a, plan.place["start", 0, (kind, a)] % 2, 0, 0, a + 1)
            for n in range(2):
                exp_block(n, n, n, lambda: act.wait_ge(scores_ready, n + 1), lambda: None)

            def step(s):
                first = s.section == "first"
                end = s.h == 7 and not s.has_next
                for i in range(BLOCKS):
                    ahead, j = divmod(i + AHEAD, BLOCKS)
                    if not (end and ahead):
                        def wait_p():
                            act.wait_ge(scores_ready, s.heads(BLOCKS, ahead, j + 1))
                            lo_wait(act, s, i)
                        def wait_h():
                            if not (first and i == 0):
                                act.wait_ge(pv_done, s.heads(BLOCKS, 0, i + (s.h == 7 and ahead)))
                        exp_block(j % 2, ring3(s, i + AHEAD), j % 2, wait_p, wait_h)
                    if i == 0 and not first:
                        copy_out(s, -1, 1)
                    if i == TT:
                        copy_out(s, 0, 0)
                    for kind, a in s.done(i):
                        take_in_step(s, kind, a)

            def copy_out(s, ahead, tc):
                act.wait_ge(pv_done, s.heads(BLOCKS, ahead, 8 * (tc + 1)))
                if not (s.section == "first" and tc == 0):
                    act.wait_ge(o_ready, s.heads(2, ahead, tc))
                nc.scalar.copy(acc[:, :], ps[PVB + tc][:, :]).then_inc(acc_ready, 1)

            def take_in_step(s, kind, a):
                bk, _ = s.bank(kind, a) if kind in ("xt", "qk", "v") else (0, 0)
                if kind == "qk":
                    take(kind, a, bk, (s.k + 1) % 2, 0, s.heads(2, 1, a + 1))
                if kind == "v":
                    take(kind, a, bk, 0, 0, s.batches(8, (8 if s.h == 7 else 0) + a + 1))
                if kind == "xt":
                    take(kind, a, bk, 0, 0, s.batches(8, 8 + a + 1))

            run(act, step)
            s = Step(act, B - 1, "last", 8, plan, B, None)
            copy_out(s, -1, 1)

        @block.vector
        def _(dve):
            raw_qk = o[:, :, :].rearrange("p a t -> p (a t)").rearrange("p (c h m) -> p c h m", c=CH, h=NH)

            def lo_part(ring2, r3, wait):
                wait()
                nc.vector.tensor_tensor(prob_l[:, r3, :], prob[:, ring2, :], prob_h[:, r3, :].bitcast(F32),
                                        ALU.subtract).then_inc(prob_l_ready, 1)

            def token_stats(x_count):
                dve.wait_ge(x_in, x_count)
                for t in range(4):
                    nc.vector.bn_stats(bn[:, t, :], xs[:, t, :]).then_inc(stat_done, 1)

            def token_mean():
                for t in range(4):
                    nc.vector.bn_aggr(mv[:, t, :], bn[:, t, :]).then_inc(stat_done, 1)

            def take_mean(bank, count, at):
                w = ps[WB + bank]
                dve.wait_ge(mean_done, count)
                nc.vector.tensor_copy(gmean[:, :], w[:, 0:4]).then_inc(stat_done, 1)
                nc.vector.tensor_tensor(dev[:, :], mv[:, :, 0], w[:, 0:4], ALU.subtract).then_inc(stat_done, 1)
                dve.wait_ge(stat_done, at(10))
                nc.vector.tensor_tensor(dev2[:, :], dev[:, :], dev[:, :], ALU.mult).then_inc(stat_done, 1)
                dve.wait_ge(stat_done, at(11))
                nc.vector.tensor_tensor(spread[:, :], dev2[:, :], mv[:, :, 1], ALU.add).then_inc(taken[bank], 1)

            def take_var(bank, count):
                dve.wait_ge(var_done, count)
                nc.vector.tensor_scalar(gvar[:, :], ps[WB + bank][:, 0:4], EPS, None, ALU.add).then_inc(taken[bank], 1)

            def norm(count):
                dve.wait_ge(rstd_ready, count)
                for t in range(4):
                    nc.vector.tensor_scalar(xs[:, t, :], xs[:, t, :], gmean[:, t:t + 1], rstd[:, t:t + 1],
                                            ALU.subtract, ALU.mult).then_inc(xn_ready, 1)

            def take(kind, a, bank, slot, count, hi_count):
                w = ps[WB + bank]
                if kind == "xt":
                    dve.wait_ge(xt_hi, count)
                    cols = slice(a * P, (a + 1) * P)
                    nc.vector.tensor_tensor(xl[:, :, cols], w[:, :].rearrange("p (c t) -> p c t", c=CH),
                                            xh[:, :, cols].bitcast(F32), ALU.subtract).then_inc(taken[bank], 1)
                if kind == "qk":
                    cols = slice(a * 512, (a + 1) * 512)
                    dve.wait_ge(qk_hi, hi_count)
                    nc.vector.tensor_tensor(q_lm[0:D, slot, cols], w[0:D, :], q_hh[0:D, slot, cols].bitcast(F32),
                                            ALU.subtract)
                    nc.vector.tensor_tensor(k_hl[D:P, slot, cols], w[D:P, :], k_h1[0:D, slot, cols].bitcast(F32),
                                            ALU.subtract).then_inc(taken[bank], 1)
                if kind == "v":
                    half, e = divmod(a, 4)
                    dve.wait_ge(v_hi, count)
                    for j in range(2):
                        for odd in range(2):
                            at = (slice(None), 2 * e + j, slice(2 * half, 2 * half + 2),
                                  slice(odd * (D + 1), odd * (D + 1) + D))
                            last = nc.vector.tensor_tensor(
                                vl[at], w[:, j * 256:(j + 1) * 256].rearrange("p (a o d) -> p o a d", o=2, d=D)[:, odd],
                                vh[at].bitcast(F32), ALU.subtract)
                    last.then_inc(taken[bank], 1)

            def take_max(j, count):
                dve.wait_ge(rows_ready, count)
                nc.vector.tensor_reduce(smax[:, j:j + 1], ps[SM + j % 2][:, :], AX.X, ALU.max).then_inc(rows_used, 1)

            def combine(half, used):
                dve.wait_ge(rows_used, used)
                nc.vector.tensor_reduce(nmax[:, 4 * half:4 * half + 4],
                                        smax[:, 8 * half:8 * half + 8].rearrange("p (t a) -> p t a", a=2),
                                        AX.X, ALU.max, negate=True).then_inc(nmax_ready, 1)

            def take_rows(half, bank, count):
                dve.wait_ge(mt_done, count)
                nc.vector.tensor_copy(mrow[:, half, :], ps[WB + bank][0:4, 0:P]).then_inc(taken[bank], 1)

            for tensor, value in ((vh, 1.0), (vl, 0.0)):
                nc.vector.memset(tensor[:, :, :, D:D + 1].bitcast(F32), value).then_inc(v_cols, 1)
            token_stats(16)
            dve.wait_ge(stat_done, 4)
            token_mean()
            dve.wait_ge(w_hi, 1)
            nc.vector.tensor_tensor(wqk_l[:, :, :, :].rearrange("p c h m -> p (c h m)"),
                                    o[:, :, :].rearrange("p a t -> p (a t)"),
                                    wqk_h[:, :, :, :].rearrange("p c h m -> p (c h m)").bitcast(F32),
                                    ALU.subtract).then_inc(w_lo, 1)
            dve.wait_ge(w_hi, 2)
            nc.vector.tensor_tensor(wv_l[:, :, :], wp[:, :, :], wv_h[:, :, :].bitcast(F32), ALU.subtract).then_inc(w_lo, 1)
            for kind, a in plan.prologue:
                bk = plan.place["start", 0, (kind, a)] % 2
                if kind == "mean":
                    if a:
                        token_stats(32)
                        dve.wait_ge(stat_done, 15)
                        token_mean()
                    take_mean(bk, a + 1, lambda n: 11 * a + n)
                elif kind == "var":
                    take_var(bk, a + 1)
                    norm(a + 1)
                elif kind == "mt":
                    take_rows(0, bk, 1)
                    for j in range(10, BLOCKS):
                        take_max(j, j + 1)
                    combine(1, BLOCKS)
                else:
                    take(kind, a, bk, 0, a + 1, a + 1)
                if (kind, a) == ("v", 1):
                    for j in range(10):
                        take_max(j, j + 1)
                        if j == 7:
                            combine(0, 8)
            for n in range(2):
                if n in POOL_BLOCKS:
                    continue
                lo_part(n, n, lambda: dve.wait_ge(prob_h_ready, n + 1))

            def step(s):
                first = s.section == "first"
                end = s.h == 7 and not s.has_next
                per_slot = max_blocks(s.h, s.has_next)
                hj = 0
                for i in range(BLOCKS):
                    ahead, j = divmod(i + AHEAD, BLOCKS)
                    token_means = s.has_next and (s.h, i) in ((3, 4), (6, 10))
                    if token_means:
                        dve.wait_ge(stat_done, s.batches(22, 22 + 11 * (s.h == 6) + 4))
                    for kind, a in s.done(i):
                        if kind == "mt":
                            take_rows(a, s.bank(kind, a)[0], s.heads(2, 0 if a else 1, 2 if a else 1))
                    for _ in range(per_slot[i - 1] if i else 0):
                        take_max(hj, s.heads(BLOCKS, 1, hj + 1))
                        hj += 1
                        if hj in (8, 16):
                            combine(hj // 8 - 1, s.heads(BLOCKS, 1, hj))
                    if j not in POOL_BLOCKS and not (end and ahead):
                        lo_part(j % 2, ring3(s, i + AHEAD),
                                lambda: dve.wait_ge(prob_h_ready, s.heads(BLOCKS, ahead, j + 1)))
                    if token_means:
                        token_mean()
                    for kind, a in s.done(i):
                        bk, _ = s.bank(kind, a)
                        if kind == "qk":
                            take(kind, a, bk, (s.k + 1) % 2, None, s.heads(2, 1, a + 1))
                        elif kind == "v":
                            take(kind, a, bk, 0, s.batches(8, (8 if s.h == 7 else 0) + a + 1), None)
                        elif kind == "xt":
                            take(kind, a, bk, 0, s.batches(8, 8 + a + 1), None)
                        elif kind == "mean":
                            take_mean(bk, s.batches(2, 2 + a + 1), lambda n: s.batches(22, 22 + 11 * a + n))
                        elif kind == "var":
                            take_var(bk, s.batches(2, 2 + a + 1))
                            norm(s.batches(2, 2 + a + 1))
                        elif kind == "proj":
                            output(s, a, bk)
                    if i == 3 and not first:
                        reciprocal(s, -1, 1)
                    if i == 11:
                        reciprocal(s, 0, 0)
                    if s.h == 3 and i == 2 and s.has_next:
                        token_stats(s.batches(32, 48))
                    if s.h == 6 and i == 8 and s.has_next:
                        token_stats(s.batches(32, 64))

            def reciprocal(s, ahead, tc):
                dve.wait_ge(den_in, s.heads(32, ahead, 16 * (tc + 1)))
                nc.vector.reciprocal(inv[:, :], den[:, :]).then_inc(inv_ready, 1)

            def output(s, t, bank):
                dve.wait_ge(proj_done, s.batches(8, t + 1))
                dve.wait_ge(res_bias, s.batches(8, t + 1))
                nc.vector.tensor_tensor(res[:, t % RES, :], ps[WB + bank][:, :], res[:, t % RES, :], ALU.add).then_inc(taken[bank], 1)

            run(dve, step)
            s = Step(dve, B - 1, "last", 8, plan, B, None)
            reciprocal(s, -1, 1)
            for t in range(TT):
                output(s, t, s.bank("proj", t)[0])

        @block.gpsimd
        def _(pool):
            pool.memset(ident[:, :], 0.0).then_inc(consts, 1)
            pool.memset(group_avg[:, :], 0.0).then_inc(consts, 1)
            pool.memset(minus_half[:, :], -0.5).then_inc(consts, 1)
            pool.wait_ge(consts, 3)
            pool.memset(k_h1[D:D + 1, :, :].bitcast(F32), 1.0).then_inc(consts, 1)
            pool.wait_ge(consts, 4)
            pool.affine_select(out=ident[:, :], in_=ident[:, :], compare_op=ALU.not_equal, fill=1.0,
                               base=0, pattern=[[-1, P]], channel_multiplier=1).then_inc(consts, 1)
            for q in range(P // PER_GROUP):
                g = slice(q * PER_GROUP, (q + 1) * PER_GROUP)
                pool.wait_ge(consts, 5 + q)
                pool.memset(group_avg[g, g], 1.0 / PER_GROUP).then_inc(consts, 1)
            pool.wait_ge(consts, 9)

            def rsqrt():
                nc.gpsimd.tensor_tensor(rstd[:, :], gvar[:, :], minus_half[:, :], ALU.pow).then_inc(rstd_ready, 1)

            for half in range(2):
                start_taken(pool, "var", half)
                rsqrt()

            def lo_part(ring2, r3, count):
                pool.wait_ge(prob_h_ready, count)
                nc.gpsimd.tensor_tensor(prob_l[:, r3, :], prob[:, ring2, :], prob_h[:, r3, :].bitcast(F32),
                                        ALU.subtract).then_inc(prob_l_pool, 1)

            lo_part(1, 1, 2)

            def normalise(s, ahead, tc):
                h = (s.h + ahead) % NH
                r = rows(h)[0]
                if s.section == "body" and s.k == 8:
                    pool.wait_ge(res_bias, s.batches(8, 3 if tc else 6))
                done_slots = 0 if s.slots is None else 8 if tc else BLOCKS
                pool.wait_ge(prob_l_pool, s.heads(per_pool, 0, sum(j < done_slots for j in POOL_BLOCKS)))
                pool.wait_ge(inv_in, s.heads(32, ahead, 16 * (tc + 1)))
                nc.gpsimd.tensor_tensor(o[r, h // 2, tc * 512:(tc + 1) * 512], acc[r, :], inv_b[r, :],
                                        ALU.mult).then_inc(o_ready, 1)
                pool.wait_ge(o_ready, s.heads(2, ahead, tc + 1))

            def add_bias(s, t):
                pool.wait_ge(res_in[t % RES], tile_count(s, t, 0))
                nc.gpsimd.tensor_tensor(res[:, t % RES, :], res[:, t % RES, :], bias[:, :], ALU.add).then_inc(res_bias, 1)

            def step(s):
                first = s.section == "first"
                end = s.h == 7 and not s.has_next
                for i in range(BLOCKS):
                    ahead, j = divmod(i + AHEAD, BLOCKS)
                    if j in POOL_BLOCKS and not (end and ahead):
                        lo_part(j % 2, ring3(s, i + AHEAD), s.heads(BLOCKS, ahead, j + 1))
                    if i == 6 and not first:
                        normalise(s, -1, 1)
                    if i == 14:
                        normalise(s, 0, 0)
                    if s.has_next and (s.h, i) in ((3, 9), (6, 13)):
                        entry_taken(pool, s, "var", 0 if s.h == 3 else 1)
                        rsqrt()
                    if s.section == "body" and s.k == 8:
                        for t, at in enumerate(PROJ_SLOTS):
                            if i == at:
                                add_bias(s, t)

            pool.wait_ge(bias_in, 16)
            run(pool, step)
            s = Step(pool, B - 1, "last", 8, plan, B, None)
            normalise(s, -1, 1)
            for t in range(TT):
                add_bias(s, t)


_INS = ["x", "L0_conv_Wq", "L0_conv_Wk", "L0_conv_Wv", "L0_conv_Wproj", "L0_conv_bproj"]


def kernel(**inputs):
    import numpy as np
    import concourse.bacc as bacc
    from concourse.bass_utils import run_bass_kernel_spmd

    nc = bacc.Bacc("TRN2", target_bir_lowering=False, num_devices=1)
    arrays, args = {}, []
    for name in _INS:
        a = np.ascontiguousarray(inputs[name])
        arrays[f"in_{name}"] = a
        args.append(nc.dram_tensor(f"in_{name}", a.shape, mybir.dt.from_np(a.dtype), kind="ExternalInput").ap())
    shape = arrays["in_x"].shape
    args.append(nc.dram_tensor("out_x", shape, F32, kind="ExternalOutput").ap())
    attention_block(nc, *args)
    r = run_bass_kernel_spmd(nc, [arrays], core_ids=[0])
    return r.results[0]["out_x"]
```

```python
from contextlib import ExitStack

import concourse.bass as bass
from concourse import mybir

F32 = mybir.dt.float32
F32R = mybir.dt.float32r
ALU = mybir.AluOpType
ACT = mybir.ActivationFunctionType
AX = mybir.AxisListType

P = 128
GROUPS = 32
EPS = 1e-5
ST, SM, PVB, WB = 0, 3, 5, 6

CHUNKS = {"qk": 4, "qn": 4, "v": 4, "xt": 4, "proj": 4, "mean": 1, "var": 1, "mt": 1}
RES = 3
BLOCKS = 16
AHEAD = 3
POOL_BLOCKS = (1, 5, 7, 9, 11, 13, 15)


def fillers(h, has_next, proj):
    slots = [[] for _ in range(BLOCKS)]
    if h == 7 and has_next:
        slots[0] += [("mt", 1, 0, 1)]
        slots[1] += [("xt", 5, 0, 4)]
        slots[2] += [("xt", 6, 0, 4)]
        slots[3] += [("xt", 7, 0, 4)]
        slots[4] += [("qk", 0, 0, 4)]
        slots[5] += [("qk", 1, 0, 4)]
        for e, s in enumerate((6, 7, 9, 10)):
            slots[s] += [("v", e, 0, 4)]
        slots[11] += [("mt", 0, 0, 1)]
        slots[12] += [("qn", 0, 0, 4)]
        slots[13] += [("qn", 1, 0, 4)]
    elif h == 6 and has_next:
        slots[0] += [("xt", 0, 0, 4)]
        slots[1] += [("mt", 1, 0, 1)]
        for t in range(1, 4):
            slots[1 + t] += [("xt", t, 0, 4)]
        slots[9] += [("mean", 1, 0, 1)]
        slots[10] += [("mt", 0, 0, 1)]
        slots[11] += [("var", 1, 0, 1)]
        slots[14] += [("xt", 4, 0, 4)]
    else:
        slots[1] += [("mt", 1, 0, 1)]
        if h in (1, 2):
            slots[3] += [("v", 4 + 2 * (h - 1), 0, 4)]
            slots[6] += [("v", 5 + 2 * (h - 1), 0, 4)]
        if h == 3 and has_next:
            slots[6] += [("mean", 0, 0, 1)]
            slots[8] += [("var", 0, 0, 1)]
        if h < 7:
            slots[10] += [("mt", 0, 0, 1)]
    if proj:
        slots[12] += [("qn", 0, 0, 4)]
        slots[13] += [("qn", 1, 0, 4)]
        for t, s in enumerate(PROJ_SLOTS):
            slots[s] += [("proj", t, 0, 4)]
    elif h < 6:
        slots[11] += [("qn", 0, 0, 3)]
        slots[12] += [("qn", 0, 3, 4), ("qn", 1, 0, 2)]
        slots[13] += [("qn", 1, 2, 4)]
    return slots


STAT_SLOTS = (1, 2, 3, 4), (4, 6, 7, 8)
NORM_SLOTS = (11, 12, 13, 14), (13, 13, 14, 14)
PROJ_SLOTS = (3, 4, 5, 6, 8, 9, 11, 14)


def max_blocks(h, has_next):
    if h == 7 and not has_next:
        return [0] * BLOCKS
    if h == 7:
        return [0] * 7 + [2] * 8 + [0]
    return [0, 1, 1, 1, 1, 1, 1, 1, 1, 2, 1, 2, 1, 1, 1, 0]


class Plan:

    def __init__(self, batches):
        self.prologue = [("mean", 0), ("var", 0)] + [("xt", t) for t in range(4)]
        self.prologue += [("mean", 1), ("var", 1)] + [("xt", t) for t in range(4, 8)]
        self.prologue += [("qk", 0), ("qk", 1), ("qn", 0), ("qn", 1), ("v", 0), ("v", 1), ("mt", 0), ("v", 2), ("v", 3)]
        self.place = {("start", 0, e): n for n, e in enumerate(self.prologue)}
        n = len(self.prologue)
        self.steps = {}
        for section, ks in (("first", [0]), ("body", range(1, 9)), ("last", range(1, 8))):
            if section == "last":
                n = body_start + self.per_batch * (batches - 1)
            if section == "body":
                body_start = n
            for k in ks:
                has_next = section != "last"
                slots = fillers(k % 8, has_next, k == 8)
                assert not slots[BLOCKS - 1]
                ends = []
                for s, slot in enumerate(slots):
                    for kind, a, lo, hi in slot:
                        if lo == 0:
                            assert len(ends) < 2 or ends[-2] < s
                            ends.append(BLOCKS)
                        if hi == CHUNKS[kind]:
                            ends[-1] = s
                self.steps[section, k] = slots
                for s in slots:
                    for kind, a, lo, hi in s:
                        if lo == 0:
                            self.place[section, k, (kind, a)] = n
                            n += 1
            if section == "body":
                self.per_batch = n - body_start
        for t in range(8):
            self.place["last", 8, ("proj", t)] = n + t
        assert self.per_batch % 2 == 0


class Step:

    def __init__(self, eng, it, section, k, plan, last_batch, bases):
        self.eng, self.it, self.section, self.k = eng, it, section, k
        self.plan, self.bases = plan, bases
        self.h = k % 8
        self.has_next = section != "last"
        self.slots = plan.steps.get((section, k))
        self.looped = section == "body"

    def at(self, per_batch, const):
        if not self.looped:
            return per_batch * self.it + const
        if per_batch not in self.bases:
            self.bases[per_batch] = self.eng.snap(self.it * per_batch)
        return self.bases[per_batch] + const

    def heads(self, per_head, ahead=0, more=0):
        return self.at(8 * per_head, per_head * (self.k + ahead) + more)

    def batches(self, per_batch, more):
        return self.at(per_batch, more)

    def bank(self, kind, arg, back=0):
        n = self.plan.place[self.section, self.k - back, (kind, arg)]
        per = self.plan.per_batch
        if self.looped:
            return n % 2, self.at(per // 2, n // 2)
        return n % 2, n // 2

    def done(self, slot):
        pieces = self.slots[slot - 1] if slot else []
        return [(kind, a) for kind, a, lo, hi in pieces if hi == CHUNKS[kind]]


def attention_block(nc, x, Wq, Wk, Wv, Wproj, bproj, out):
    B, C, H_, W_ = x.shape
    T = H_ * W_
    NH, _, D = Wq.shape
    CH = C // P
    TT = T // P
    TC = T // 512
    SCALE = D ** -0.5
    PER_GROUP = T // GROUPS
    assert (C, T, NH, D, CH, TT, TC) == (512, 1024, 8, 64, 4, 8, 2)
    plan = Plan(B)

    xv = x.rearrange("b c h w -> b (c h w)").rearrange("b (k p c) -> b p k c", p=P, c=C)
    ov = out.rearrange("b c h w -> b (c h w)").rearrange("b (k p c) -> b p k c", p=P, c=C)
    inv_dram = nc.dram_tensor("inv_dram", (1, 512), F32).ap()

    with ExitStack() as ctx:
        def sb(name, shape, dt=F32):
            return ctx.enter_context(nc.sbuf_tensor(name, shape, dt))

        def sem(name):
            return ctx.enter_context(nc.semaphore(name))

        wqk_h = sb("wqk_h", [P, CH, NH, P], F32R)
        wqk_l = sb("wqk_l", [P, CH, NH, P], F32R)
        wv_h = sb("wv_h", [P, CH, C], F32R)
        wv_l = sb("wv_l", [P, CH, C], F32R)
        wp = sb("wp", [P, CH, C])
        bias = sb("bias", [P, C])
        ident = sb("ident", [P, P])
        group_avg = sb("group_avg", [P, P])
        xh = sb("xh", [P, CH, T], F32R)
        xl = sb("xl", [P, CH, T], F32R)
        VW = 2 * D + 1
        vh = sb("vh", [P, TT, NH // 2, VW], F32R)
        vl = sb("vl", [P, TT, NH // 2, VW], F32R)
        q_hh = sb("q_hh", [P, 2, T], F32R)
        q_lm = sb("q_lm", [P, 2, T], F32R)
        k_hl = sb("k_hl", [P, 2, T], F32R)
        k_h1 = sb("k_h1", [P, 2, T], F32R)
        prob = sb("prob", [P, 2, 512])
        prob_h = sb("prob_h", [P, 3, 512], F32R)
        prob_l = sb("prob_l", [P, 3, 512], F32R)
        acc = sb("acc", [P, 2, 512])
        inv_b = sb("inv_b", [P, 512])
        den = sb("den", [32, 16])
        inv = sb("inv", [32, 16])
        o = sb("o", [P, NH // 2, T])
        xs = sb("xs", [P, 4, C])
        res = sb("res", [P, RES, C])
        smax = sb("smax", [P, BLOCKS])
        nmax = sb("nmax", [P, TT])
        mrow = q_lm[96:100, 0, 0:2 * P].rearrange("p (a q) -> p a q", a=2)
        bn = sb("bn", [P, 4, 6])
        mv = sb("mv", [P, 4, 2])
        gmean = sb("gmean", [P, 4])
        dev = sb("dev", [P, 4])
        dev2 = sb("dev2", [P, 4])
        spread = sb("spread", [P, 4])
        gvar = sb("gvar", [P, 4])
        rstd = sb("rstd", [P, 4])
        minus_half = sb("minus_half", [P, 4])

        ps = [ctx.enter_context(nc.psum_tensor(f"bank{n}", [P, 512], F32)) for n in range(8)]

        weights_in = sem("weights_in")
        wv_in = sem("wv_in")
        wp_in = sem("wp_in")
        bias_in = sem("bias_in")
        x_in = [sem(f"x_in{t}") for t in range(4)]
        res_in = [sem(f"res_in{n}") for n in range(RES)]
        y_out = [sem(f"y_out{n}") for n in range(RES)]
        den_in = sem("den_in")
        inv_out = sem("inv_out")
        inv_in = sem("inv_in")
        mrow_in = [sem("mrow_in0"), sem("mrow_in1")]
        w_hi = sem("w_hi")
        w_lo = sem("w_lo")
        consts = sem("consts")
        v_cols = sem("v_cols")
        stat_done = sem("stat_done")
        rstd_ready = sem("rstd_ready")
        xn_ready = sem("xn_ready")
        mean_done = sem("mean_done")
        var_done = sem("var_done")
        xt_done = sem("xt_done")
        qk_done = sem("qk_done")
        v_done = sem("v_done")
        mt_done = sem("mt_done")
        proj_done = sem("proj_done")
        xt_hi = sem("xt_hi")
        qk_hi = sem("qk_hi")
        k_split = sem("k_split")
        qk_twice = [[sem(f"qk_twice{slot}{a}") for a in range(2)] for slot in range(2)]
        v_hi = sem("v_hi")
        taken = [sem("taken0"), sem("taken1")]
        scores_ready = sem("scores_ready")
        rows_ready = sem("rows_ready")
        rows_used = sem("rows_used")
        nmax_ready = sem("nmax_ready")
        prob_ready = sem("prob_ready")
        prob_h_ready = sem("prob_h_ready")
        prob_l_ready = sem("prob_l_ready")
        prob_l_pool = sem("prob_l_pool")
        pv_done = sem("pv_done")
        acc_ready = sem("acc_ready")
        inv_ready = sem("inv_ready")
        o_ready = sem("o_ready")
        res_bias = sem("res_bias")

        per_pool = len(POOL_BLOCKS)
        per_dve = BLOCKS - per_pool

        def lo_wait(eng, s, i):
            ahead, i = divmod(i, BLOCKS)
            if i in POOL_BLOCKS:
                eng.wait_ge(prob_l_pool, s.heads(per_pool, ahead, POOL_BLOCKS.index(i) + 1))
            else:
                n = sum(j not in POOL_BLOCKS for j in range(i + 1))
                eng.wait_ge(prob_l_ready, s.heads(per_dve, ahead, n))

        def entry_taken(eng, s, kind, a, back=0):
            bank, before = s.bank(kind, a, back)
            eng.wait_ge(taken[bank], before + 1)

        def start_taken(eng, kind, a):
            n = plan.place["start", 0, (kind, a)]
            eng.wait_ge(taken[n % 2], n // 2 + 1)

        def tile_count(s, t, credit=16):
            r = t % RES
            return s.batches(16 * len(range(r, TT, RES)), credit + 16 * (t // RES + 1))

        def rows(h):
            return (slice(0, D), D) if h % 2 == 0 else (slice(D, P), D - 1)

        def run(eng, step):
            step(Step(eng, 0, "first", 0, plan, B, None))
            with eng.Fori(0, B - 1) as it:
                bases = {}
                for k in range(1, 9):
                    step(Step(eng, it, "body", k, plan, B, bases))
            for k in range(1, 8):
                step(Step(eng, B - 1, "last", k, plan, B, None))

        def ring3(s, i):
            return (BLOCKS * s.h + i) % (BLOCKS * NH) % 3

        def early(s, i):
            return int(s.h == 7 and i + AHEAD - BLOCKS in (0, 1))

        block = ctx.enter_context(nc.Block())

        @block.sync
        def _(sp):
            raw_qk = o[:, :, :].rearrange("p a t -> p (a t)").rearrange("p (c h m) -> p c h m", c=CH, h=NH)
            for t in range(4):
                sp.dma_start(xs[:, t, :], xv[0, :, t, :]).then_inc(x_in[t], 16)
            for r in range(RES):
                sp.sem_inc(y_out[r], 16)
            for c in range(CH):
                for half, w in ((0, Wq), (1, Wk)):
                    sp.dma_start(raw_qk[:, c, :, half * D:(half + 1) * D],
                                 w[:, c * P:(c + 1) * P, :].rearrange("h p d -> p h d")).then_inc(weights_in, 16)
                sp.dma_start(wp[:, c, :].rearrange("p (h d) -> p h d", h=NH),
                             Wv[:, c * P:(c + 1) * P, :].rearrange("h p d -> p h d")).then_inc(wv_in, 16)
            sp.dma_start(bias[:, :], bproj.partition_broadcast(P)).then_inc(bias_in, 16)
            for t in range(4):
                sp.wait_ge(xt_done, t + 1)
                sp.dma_start(xs[:, t, :], xv[0, :, 4 + t, :]).then_inc(x_in[t], 16)
            sp.wait_ge(w_lo, 2)
            sp.dma_start(wp[:, :, :], Wproj.rearrange("(c p) n -> p c n", p=P)).then_inc(wp_in, 16)

            def max_row(half, slot):
                sp.dma_start(q_lm[D:D + 1, slot, half * 512:(half + 1) * 512].bitcast(F32),
                             mrow[:, half, :].bitcast(F32)).then_inc(mrow_in[half], 16)

            def twice(a, slot, count):
                sp.wait_ge(qk_hi, count)
                cols = slice(a * 512, (a + 1) * 512)
                sp.dma_start(q_hh[D:P, slot, cols].bitcast(F32),
                             q_hh[0:D, slot, cols].bitcast(F32)).then_inc(qk_twice[slot][a], 16)
                sp.dma_start(k_hl[0:D, slot, cols].bitcast(F32),
                             k_h1[0:D, slot, cols].bitcast(F32)).then_inc(qk_twice[slot][a], 16)

            twice(0, 0, 1)
            twice(1, 0, 2)
            twice(0, 1, 3)
            twice(1, 1, 4)
            start_taken(sp, "mt", 0)
            max_row(0, 0)

            def den_to_square(s, ahead, tc):
                sp.wait_ge(acc_ready, s.heads(2, ahead, tc + 1))
                r = rows(s.h + ahead)[1]
                sp.dma_start(den[:, :], acc[r:r + 1, tc, :]).then_inc(den_in, 16)

            def inv_to_rows(s, ahead, tc):
                sp.wait_ge(inv_ready, s.heads(2, ahead, tc + 1))
                sp.dma_start(inv_dram[0:1, :].rearrange("a (p f) -> (a p) f", p=32), inv[:, :]).then_inc(inv_out, 16)
                sp.wait_ge(inv_out, s.heads(32, ahead, 16 * (tc + 1)))
                sp.dma_start(inv_b[rows(s.h + ahead)[0], :],
                             inv_dram[0, :].partition_broadcast(D)).then_inc(inv_in, 16)

            def residual(s, t, b):
                sp.wait_ge(y_out[t % RES], tile_count(s, t - RES))
                sp.dma_start(res[:, t % RES, :], xv[b, :, t, :]).then_inc(res_in[t % RES], 16)

            def store(s, t, b):
                entry_taken(sp, s, "proj", t)
                sp.dma_start(ov[b, :, t, :], res[:, t % RES, :]).then_inc(y_out[t % RES], 16)

            def step(s):
                first = s.section == "first"
                for i in range(BLOCKS):
                    if i == 1 and not first:
                        den_to_square(s, -1, 1)
                    if i == 2:
                        entry_taken(sp, s, "mt", 1)
                        max_row(1, s.k % 2)
                    for kind, a in s.done(i):
                        if kind == "qk":
                            twice(a, (s.k + 1) % 2, s.heads(2, 1, a + 1))
                        if kind == "qn":
                            twice(a, s.k % 2, s.heads(2, 2, a + 1))
                    if i == 4 and not first:
                        inv_to_rows(s, -1, 1)
                    if i == 9:
                        den_to_square(s, 0, 0)
                    if i == 11 and not (s.h == 7 and not s.has_next):
                        entry_taken(sp, s, "mt", 0)
                        max_row(0, (s.k + 1) % 2)
                    if i == 12:
                        inv_to_rows(s, 0, 0)
                    if s.h == 2 and i == 8 and s.has_next:
                        sp.wait_ge(xt_done, s.batches(8, 8))
                        for t in range(4):
                            sp.dma_start(xs[:, t, :], xv[s.it + 1, :, t, :]).then_inc(x_in[t], 16)
                    for kind, a in s.done(i):
                        if kind == "xt" and a < 4:
                            sp.wait_ge(xt_done, s.batches(8, 8 + a + 1))
                            sp.dma_start(xs[:, a, :], xv[s.it + 1, :, 4 + a, :]).then_inc(x_in[a], 16)
                    if s.section == "body" and s.k == 8:
                        if i < RES:
                            residual(s, i, s.it)
                        for t, at in enumerate(PROJ_SLOTS):
                            if i == at + 1:
                                store(s, t, s.it)
                                if 1 <= t <= TT - RES:
                                    residual(s, t + RES - 1, s.it)

            run(sp, step)
            s = Step(sp, B - 1, "last", 8, plan, B, None)
            den_to_square(s, -1, 1)
            for t in range(RES):
                residual(s, t, B - 1)
            inv_to_rows(s, -1, 1)
            for t in range(TT):
                store(s, t, B - 1)
                if 1 <= t <= TT - RES:
                    residual(s, t + RES - 1, B - 1)
            for t in range(TT - RES, TT):
                sp.wait_ge(y_out[t % RES], tile_count(s, t))

        @block.tensor
        def _(pe):
            def split_product(bank, cols, pairs, start, stop):
                n = len(pairs)
                for j, (w, m) in enumerate(pairs):
                    last = nc.tensor.matmul(ps[bank][:, cols], w, m, start=start and j == 0,
                                            stop=stop and j == n - 1)
                return last

            def entry(kind, a, lo, hi, bank, before, s_h, s_slot, wait):
                w = ps[WB + bank]
                if lo == 0 and before is not None:
                    pe.wait_ge(taken[bank], before)
                wait()
                if kind in ("qk", "qn"):
                    cols = slice(a * 512, (a + 1) * 512)
                    for c in range(lo, hi):
                        last = split_product(WB + bank, slice(0, 512),
                                             [(wqk_h[:, c, s_h, :], xh[:, c, cols]),
                                              (wqk_l[:, c, s_h, :], xh[:, c, cols]),
                                              (wqk_h[:, c, s_h, :], xl[:, c, cols])], c == 0, c == CH - 1)
                    if hi == CH:
                        last.then_inc(qk_done, 1)
                elif kind == "v":
                    half, e = divmod(a, 4)
                    vcols = slice(half * 256, (half + 1) * 256)
                    for j in range(2):
                        t = slice((2 * e + j) * P, (2 * e + j + 1) * P)
                        for c in range(CH):
                            last = split_product(WB + bank, slice(j * 256, (j + 1) * 256),
                                                 [(xh[:, c, t], wv_h[:, c, vcols]),
                                                  (xh[:, c, t], wv_l[:, c, vcols]),
                                                  (xl[:, c, t], wv_h[:, c, vcols])], c == 0, c == CH - 1)
                    last.then_inc(v_done, 1)
                elif kind == "xt":
                    for c in range(CH):
                        last = nc.tensor.transpose(w[:, c * P:(c + 1) * P], xs[:, a % 4, c * P:(c + 1) * P],
                                                   ident[:, :])
                    last.then_inc(xt_done, 1)
                elif kind == "mean":
                    nc.tensor.matmul(w[:, 0:4], group_avg[:, :], mv[:, :, 0], start=True, stop=True).then_inc(mean_done, 1)
                elif kind == "var":
                    nc.tensor.matmul(w[:, 0:4], group_avg[:, :], spread[:, :], start=True, stop=True).then_inc(var_done, 1)
                elif kind == "mt":
                    nc.tensor.matmul(w[0:4, 0:P], nmax[:, a * 4:(a + 1) * 4], ident[:, :],
                                     start=True, stop=True).then_inc(mt_done, 1)
                elif kind == "proj":
                    for c in range(CH):
                        last = nc.tensor.matmul(w[:, :], o[:, c, a * P:(a + 1) * P], wp[:, c, :],
                                                start=c == 0, stop=c == CH - 1)
                    last.then_inc(proj_done, 1)

            def scores(slot, i, n_bank, wait):
                tc, t = divmod(i, TT)
                keys, queries = slice(t * P, (t + 1) * P), slice(tc * 512, (tc + 1) * 512)
                wait()
                s_bank = ps[ST + n_bank]
                nc.tensor.matmul(s_bank[:, :], k_hl[:, slot, keys], q_hh[:, slot, queries], start=True, stop=False)
                nc.tensor.matmul(s_bank[:, :], k_h1[0:D + 1, slot, keys], q_lm[0:D + 1, slot, queries],
                                 start=False, stop=True).then_inc(scores_ready, 1)

            def row_scores(slot, j):
                t, half = divmod(j, 2)
                nc.tensor.matmul(ps[SM + j % 2][:, :], q_hh[:, slot, t * P:(t + 1) * P],
                                 k_hl[:, slot, half * 512:(half + 1) * 512], start=True, stop=True).then_inc(rows_ready, 1)

            nothing = lambda: None
            n = 0

            def start_entry(kind, a, h=0, wait=nothing):
                pos = plan.place["start", 0, (kind, a)]
                before = pos // 2 if pos >= 2 else None
                entry(kind, a, 0, 4 if kind in ("qk", "qn", "v", "xt") else 1, pos % 2, before, h, 0, wait)

            pe.wait_ge(consts, 9)
            for half in range(2):
                start_entry("mean", half, wait=lambda: pe.wait_ge(stat_done, 11 * half + 8))
                start_entry("var", half, wait=lambda: start_taken(pe, "mean", half))
                for t in range(4 * half, 4 * half + 4):
                    start_entry("xt", t, wait=lambda: pe.wait_ge(xn_ready, t + 1))
            pe.wait_ge(w_hi, 2)
            pe.wait_ge(w_lo, 2)
            for tc in range(2):
                for t in range(4 * tc + 2, 4 * tc + 4):
                    start_taken(pe, "xt", t)
                start_entry("qk", tc)
            for tc in range(2):
                start_entry("qn", tc, 1)
            start_entry("v", 0)
            start_entry("v", 1)
            for tc in range(2):
                start_taken(pe, "qk", tc)
                pe.wait_ge(qk_twice[0][tc], 32)
            for j in range(BLOCKS):
                if j >= 2:
                    pe.wait_ge(rows_used, j - 1)
                row_scores(0, j)
                if j == 9:
                    start_entry("mt", 0, wait=lambda: pe.wait_ge(nmax_ready, 1))
            start_entry("v", 2)
            start_entry("v", 3)
            scores(0, 0, 0, lambda: pe.wait_ge(mrow_in[0], 16))
            scores(0, 1, 1, nothing)
            scores(0, 2, 2, nothing)
            pe.wait_ge(v_cols, 2)
            pe.wait_ge(wp_in, 16)

            def other_work(s, i):
                for kind, a, lo, hi in s.slots[i]:
                    bk, before = s.bank(kind, a)

                    def wait():
                        if kind == "xt":
                            pe.wait_ge(xn_ready, s.batches(8, 8 + a + 1))
                        if kind == "mean":
                            pe.wait_ge(stat_done, s.batches(22, 22 + 11 * a + 8))
                        if kind == "var":
                            entry_taken(pe, s, "mean", a)
                        if kind == "mt":
                            pe.wait_ge(nmax_ready, s.heads(2, 0 if a else 1, 2 if a else 1))
                        if kind == "proj" and a in (0, 4):
                            pe.wait_ge(o_ready, s.heads(2, 0, -1 if a == 0 else 0))
                    entry(kind, a, lo, hi, bk, before, (s.h + (2 if kind == "qn" else 1)) % NH, 0, wait)
                per_slot = max_blocks(s.h, s.has_next)
                for j in range(sum(per_slot[:i]), sum(per_slot[:i + 1])):
                    if j == 0:
                        pe.wait_ge(k_split, s.heads(2, 1, 2))
                        for a in range(2):
                            pe.wait_ge(qk_twice[(s.k + 1) % 2][a], s.at(16 * NH, 32 * ((s.k + 1) // 2 + 1)))
                    pe.wait_ge(rows_used, s.heads(BLOCKS, 1, j - 1))
                    row_scores((s.k + 1) % 2, j)

            def step(s):
                first = s.section == "first"
                end = s.h == 7 and not s.has_next
                for i in range(BLOCKS):
                    ahead, j = divmod(i + AHEAD, BLOCKS)
                    if not (end and ahead):
                        def wait():
                            pe.wait_ge(prob_h_ready, s.heads(BLOCKS, 0, i + 1 + early(s, i)))
                            if j == 0:
                                pe.wait_ge(mrow_in[0], s.heads(16, 1, 16))
                            if j == TT:
                                pe.wait_ge(mrow_in[1], s.heads(16, 0, 16))
                        scores((s.k + ahead) % 2, j, ring3(s, i + AHEAD), wait)
                    if i in (0, TT):
                        other_work(s, i)
                    tc, t = divmod(i, TT)
                    pair = s.h // 2
                    if t == 0 and not (first and tc == 0):
                        pe.wait_ge(acc_ready, s.heads(2, 0, tc))
                    if tc == 0 and t % 2 == 0 and s.h in (0, 4):
                        if first:
                            start_taken(pe, "v", t // 2)
                        elif s.h == 0:
                            entry_taken(pe, s, "v", t // 2, back=1)
                        else:
                            entry_taken(pe, s, "v", 4 + t // 2, back=3 - t // 4)
                    lo_wait(pe, s, i)
                    ring = ring3(s, i)
                    c0 = 0 if s.h % 2 == 0 else 1
                    v_hi_op, v_lo_op = vh[:, t, pair, c0:c0 + P], vl[:, t, pair, c0:c0 + P]
                    bank = PVB
                    nc.tensor.matmul(ps[bank][:, :], v_hi_op, prob_h[:, ring, :], start=t == 0, stop=False)
                    nc.tensor.matmul(ps[bank][:, :], v_lo_op, prob_h[:, ring, :], start=False, stop=False)
                    nc.tensor.matmul(ps[bank][:, :], v_hi_op, prob_l[:, ring, :],
                                     start=False, stop=t == TT - 1).then_inc(pv_done, 1)
                    if i not in (0, TT):
                        other_work(s, i)

            run(pe, step)
            s = Step(pe, B - 1, "last", 8, plan, B, None)
            pe.wait_ge(o_ready, 2 * NH * B)
            for t in range(TT):
                bk, before = s.bank("proj", t)
                entry("proj", t, 0, 4, bk, before, 0, 0, nothing)

        @block.scalar
        def _(act):
            raw_qk = o[:, :, :].rearrange("p a t -> p (a t)").rearrange("p (c h m) -> p c h m", c=CH, h=NH)

            def exp_to(out, bank, done):
                nc.scalar.activation(out, ps[ST + bank][:, :], ACT.Exp, scale=SCALE).then_inc(done, 1)

            def take(kind, a, bank, slot, h, count):
                w = ps[WB + bank]
                if kind == "xt":
                    act.wait_ge(xt_done, count)
                    nc.scalar.copy(xh[:, :, a * P:(a + 1) * P],
                                   w[:, :].rearrange("p (c t) -> p c t", c=CH)).then_inc(xt_hi, 1)
                if kind in ("qk", "qn"):
                    cols = slice(a * 512, (a + 1) * 512)
                    act.wait_ge(qk_done, count)
                    nc.scalar.copy(q_hh[0:D, slot, cols], w[0:D, :])
                    nc.scalar.copy(k_h1[0:D, slot, cols], w[D:P, :]).then_inc(qk_hi, 1)
                if kind == "v":
                    half, e = divmod(a, 4)
                    act.wait_ge(v_done, count)
                    for j in range(2):
                        for odd in range(2):
                            last = nc.scalar.copy(
                                vh[:, 2 * e + j, 2 * half:2 * half + 2, odd * (D + 1):odd * (D + 1) + D],
                                w[:, j * 256:(j + 1) * 256].rearrange("p (a o d) -> p o a d", o=2, d=D)[:, odd])
                    last.then_inc(v_hi, 1)

            act.wait_ge(weights_in, 128)
            nc.scalar.copy(wqk_h[:, :, :, :], raw_qk).then_inc(w_hi, 1)
            act.wait_ge(wv_in, 64)
            nc.scalar.copy(wv_h[:, :, :], wp[:, :, :]).then_inc(w_hi, 1)
            act.wait_ge(v_cols, 2)
            for kind, a in plan.prologue:
                if kind in ("xt", "qk", "qn", "v"):
                    qn = kind == "qn"
                    take(kind, a, plan.place["start", 0, (kind, a)] % 2, int(qn), 0, a + (3 if qn else 1))
            for n in range(AHEAD):
                act.wait_ge(scores_ready, n + 1)
                if n == 2:
                    act.wait_ge(prob_l_ready, 1)
                exp_to(prob[:, n % 2, :], n, prob_ready)
                exp_to(prob_h[:, n, :], n, prob_h_ready)

            def step(s):
                first = s.section == "first"
                end = s.h == 7 and not s.has_next
                for i in range(BLOCKS):
                    ahead, j = divmod(i + AHEAD, BLOCKS)
                    late = s.h == 7 and i in (13, 14)
                    if late:
                        for kind, a in s.done(i):
                            take_in_step(s, kind, a)
                    if not (end and ahead):
                        r3 = ring3(s, i + AHEAD)
                        act.wait_ge(scores_ready, s.heads(BLOCKS, ahead, j + 1))
                        lo_wait(act, s, i + 1)
                        exp_to(prob[:, j % 2, :], r3, prob_ready)
                    if i % TT == TT - 1:
                        copy_out(s, i // TT)
                    if not (end and ahead):
                        act.wait_ge(pv_done, s.heads(BLOCKS, 0, i + 1 + early(s, i)))
                        exp_to(prob_h[:, r3, :], r3, prob_h_ready)
                    if not late:
                        for kind, a in s.done(i):
                            take_in_step(s, kind, a)

            def copy_out(s, tc):
                act.wait_ge(pv_done, s.heads(BLOCKS, 0, 8 * (tc + 1)))
                if s.section != "first":
                    act.wait_ge(o_ready, s.heads(2, 0, tc - 1))
                nc.scalar.copy(acc[:, tc, :], ps[PVB][:, :]).then_inc(acc_ready, 1)

            def take_in_step(s, kind, a):
                bk, _ = s.bank(kind, a) if kind in ("xt", "qk", "qn", "v") else (0, 0)
                if kind == "qk":
                    take(kind, a, bk, (s.k + 1) % 2, 0, s.heads(2, 1, a + 1))
                if kind == "qn":
                    take(kind, a, bk, s.k % 2, 0, s.heads(2, 2, a + 1))
                if kind == "v":
                    take(kind, a, bk, 0, 0, s.batches(8, (8 if s.h == 7 else 0) + a + 1))
                if kind == "xt":
                    take(kind, a, bk, 0, 0, s.batches(8, 8 + a + 1))

            run(act, step)

        @block.vector
        def _(dve):
            raw_qk = o[:, :, :].rearrange("p a t -> p (a t)").rearrange("p (c h m) -> p c h m", c=CH, h=NH)

            def lo_part(ring2, r3, wait):
                wait()
                nc.vector.tensor_tensor(prob_l[:, r3, :], prob[:, ring2, :], prob_h[:, r3, :].bitcast(F32),
                                        ALU.subtract).then_inc(prob_l_ready, 1)

            def token_stats(t, x_count):
                if True:
                    dve.wait_ge(x_in[t], x_count)
                    nc.vector.bn_stats(bn[:, t, :], xs[:, t, :]).then_inc(stat_done, 1)

            def token_mean():
                for t in range(4):
                    nc.vector.bn_aggr(mv[:, t, :], bn[:, t, :]).then_inc(stat_done, 1)

            def take_mean(bank, count, at):
                w = ps[WB + bank]
                dve.wait_ge(mean_done, count)
                nc.vector.tensor_copy(gmean[:, :], w[:, 0:4]).then_inc(stat_done, 1)
                nc.vector.tensor_tensor(dev[:, :], mv[:, :, 0], w[:, 0:4], ALU.subtract).then_inc(stat_done, 1)
                dve.wait_ge(stat_done, at(10))
                nc.vector.tensor_tensor(dev2[:, :], dev[:, :], dev[:, :], ALU.mult).then_inc(stat_done, 1)
                dve.wait_ge(stat_done, at(11))
                nc.vector.tensor_tensor(spread[:, :], dev2[:, :], mv[:, :, 1], ALU.add).then_inc(taken[bank], 1)

            def take_var(bank, count):
                dve.wait_ge(var_done, count)
                nc.vector.tensor_scalar(gvar[:, :], ps[WB + bank][:, 0:4], EPS, None, ALU.add).then_inc(taken[bank], 1)

            def norm(t, count):
                if True:
                    dve.wait_ge(rstd_ready, count)
                    nc.vector.tensor_scalar(xs[:, t, :], xs[:, t, :], gmean[:, t:t + 1], rstd[:, t:t + 1],
                                            ALU.subtract, ALU.mult).then_inc(xn_ready, 1)

            def take(kind, a, bank, slot, count, hi_count):
                w = ps[WB + bank]
                if kind == "xt":
                    dve.wait_ge(xt_hi, count)
                    cols = slice(a * P, (a + 1) * P)
                    nc.vector.tensor_tensor(xl[:, :, cols], w[:, :].rearrange("p (c t) -> p c t", c=CH),
                                            xh[:, :, cols].bitcast(F32), ALU.subtract).then_inc(taken[bank], 1)
                if kind in ("qk", "qn"):
                    cols = slice(a * 512, (a + 1) * 512)
                    dve.wait_ge(qk_hi, hi_count)
                    nc.vector.tensor_tensor(k_hl[D:P, slot, cols], w[D:P, :], k_h1[0:D, slot, cols].bitcast(F32),
                                            ALU.subtract).then_inc(k_split, 1)
                    nc.vector.tensor_tensor(q_lm[0:D, slot, cols], w[0:D, :], q_hh[0:D, slot, cols].bitcast(F32),
                                            ALU.subtract).then_inc(taken[bank], 1)
                if kind == "v":
                    half, e = divmod(a, 4)
                    dve.wait_ge(v_hi, count)
                    for j in range(2):
                        for odd in range(2):
                            at = (slice(None), 2 * e + j, slice(2 * half, 2 * half + 2),
                                  slice(odd * (D + 1), odd * (D + 1) + D))
                            last = nc.vector.tensor_tensor(
                                vl[at], w[:, j * 256:(j + 1) * 256].rearrange("p (a o d) -> p o a d", o=2, d=D)[:, odd],
                                vh[at].bitcast(F32), ALU.subtract)
                    last.then_inc(taken[bank], 1)

            def take_max(j, count):
                dve.wait_ge(rows_ready, count)
                nc.vector.tensor_reduce(smax[:, j:j + 1], ps[SM + j % 2][:, :], AX.X, ALU.max).then_inc(rows_used, 1)

            def combine(half, used):
                dve.wait_ge(rows_used, used)
                nc.vector.tensor_reduce(nmax[:, 4 * half:4 * half + 4],
                                        smax[:, 8 * half:8 * half + 8].rearrange("p (t a) -> p t a", a=2),
                                        AX.X, ALU.max, negate=True).then_inc(nmax_ready, 1)

            def take_rows(half, bank, count):
                dve.wait_ge(mt_done, count)
                nc.vector.tensor_copy(mrow[:, half, :], ps[WB + bank][0:4, 0:P]).then_inc(taken[bank], 1)

            for tensor, value in ((vh, 1.0), (vl, 0.0)):
                nc.vector.memset(tensor[:, :, :, D:D + 1].bitcast(F32), value).then_inc(v_cols, 1)
            for t in range(4):
                token_stats(t, 16)
            dve.wait_ge(stat_done, 4)
            token_mean()
            dve.wait_ge(w_hi, 1)
            nc.vector.tensor_tensor(wqk_l[:, :, :, :].rearrange("p c h m -> p (c h m)"),
                                    o[:, :, :].rearrange("p a t -> p (a t)"),
                                    wqk_h[:, :, :, :].rearrange("p c h m -> p (c h m)").bitcast(F32),
                                    ALU.subtract).then_inc(w_lo, 1)
            dve.wait_ge(w_hi, 2)
            nc.vector.tensor_tensor(wv_l[:, :, :], wp[:, :, :], wv_h[:, :, :].bitcast(F32), ALU.subtract).then_inc(w_lo, 1)
            for kind, a in plan.prologue:
                bk = plan.place["start", 0, (kind, a)] % 2
                if kind == "mean":
                    if a:
                        for t in range(4):
                            token_stats(t, 32)
                        dve.wait_ge(stat_done, 15)
                        token_mean()
                    take_mean(bk, a + 1, lambda n: 11 * a + n)
                elif kind == "var":
                    take_var(bk, a + 1)
                    for t in range(4):
                        norm(t, a + 1)
                elif kind == "mt":
                    take_rows(0, bk, 1)
                    for j in range(10, BLOCKS):
                        take_max(j, j + 1)
                    combine(1, BLOCKS)
                else:
                    qn = kind == "qn"
                    take(kind, a, bk, int(qn), a + 1, a + (3 if qn else 1))
                if (kind, a) == ("v", 1):
                    for j in range(10):
                        take_max(j, j + 1)
                        if j == 7:
                            combine(0, 8)
            for n in range(AHEAD):
                if n in POOL_BLOCKS:
                    continue
                lo_part(n % 2, n, lambda: dve.wait_ge(prob_h_ready, n + 1))

            def step(s):
                first = s.section == "first"
                end = s.h == 7 and not s.has_next
                per_slot = max_blocks(s.h, s.has_next)
                hj = 0
                for i in range(BLOCKS):
                    ahead, j = divmod(i + AHEAD, BLOCKS)
                    if s.h in (3, 6) and s.has_next:
                        half = int(s.h == 6)
                        for t in range(4):
                            if STAT_SLOTS[half][t] == i:
                                token_stats(t, s.batches(32, 48 + 16 * half))
                    token_means = s.has_next and (s.h, i) in ((3, 5), (6, 8))
                    if token_means:
                        dve.wait_ge(stat_done, s.batches(22, 22 + 11 * (s.h == 6) + 4))
                    for kind, a in s.done(i):
                        if kind == "mt":
                            take_rows(a, s.bank(kind, a)[0], s.heads(2, 0 if a else 1, 2 if a else 1))
                    for _ in range(per_slot[i - 1] if i else 0):
                        take_max(hj, s.heads(BLOCKS, 1, hj + 1))
                        hj += 1
                        if hj in (8, 16):
                            combine(hj // 8 - 1, s.heads(BLOCKS, 1, hj))
                    if s.h == 7 and i == 14 and not end:
                        lo_part(0, ring3(s, 13 + AHEAD), lambda: dve.wait_ge(prob_h_ready, s.heads(BLOCKS, 1, 1)))
                    if j not in POOL_BLOCKS and not (end and ahead) and not (s.h == 7 and i == 13):
                        lo_part(j % 2, ring3(s, i + AHEAD),
                                lambda: dve.wait_ge(prob_h_ready, s.heads(BLOCKS, ahead, j + 1)))
                    if token_means:
                        token_mean()
                    for kind, a in s.done(i):
                        bk, _ = s.bank(kind, a)
                        if kind == "qk":
                            take(kind, a, bk, (s.k + 1) % 2, None, s.heads(2, 1, a + 1))
                        elif kind == "qn":
                            take(kind, a, bk, s.k % 2, None, s.heads(2, 2, a + 1))
                        elif kind == "v":
                            take(kind, a, bk, 0, s.batches(8, (8 if s.h == 7 else 0) + a + 1), None)
                        elif kind == "xt":
                            take(kind, a, bk, 0, s.batches(8, 8 + a + 1), None)
                        elif kind == "mean":
                            take_mean(bk, s.batches(2, 2 + a + 1), lambda n: s.batches(22, 22 + 11 * a + n))
                        elif kind == "var":
                            take_var(bk, s.batches(2, 2 + a + 1))
                        elif kind == "proj":
                            output(s, a, bk)
                    if i == 3 and not first:
                        reciprocal(s, -1, 1)
                    if i == 11:
                        reciprocal(s, 0, 0)
                    if s.h in (3, 6) and s.has_next:
                        half = int(s.h == 6)
                        for t in range(4):
                            if NORM_SLOTS[half][t] == i:
                                norm(t, s.batches(2, 2 + half + 1))

            def reciprocal(s, ahead, tc):
                if not (s.section == "first" and tc == 0):
                    dve.wait_ge(o_ready, s.heads(2, ahead, tc))
                dve.wait_ge(den_in, s.heads(32, ahead, 16 * (tc + 1)))
                nc.vector.reciprocal(inv[:, :], den[:, :]).then_inc(inv_ready, 1)

            def output(s, t, bank):
                dve.wait_ge(proj_done, s.batches(8, t + 1))
                dve.wait_ge(res_bias, s.batches(8, t + 1))
                nc.vector.tensor_tensor(res[:, t % RES, :], ps[WB + bank][:, :], res[:, t % RES, :], ALU.add).then_inc(taken[bank], 1)

            run(dve, step)
            s = Step(dve, B - 1, "last", 8, plan, B, None)
            reciprocal(s, -1, 1)
            for t in range(TT):
                output(s, t, s.bank("proj", t)[0])

        @block.gpsimd
        def _(pool):
            pool.memset(ident[:, :], 0.0).then_inc(consts, 1)
            pool.memset(group_avg[:, :], 0.0).then_inc(consts, 1)
            pool.memset(minus_half[:, :], -0.5).then_inc(consts, 1)
            pool.wait_ge(consts, 3)
            pool.memset(k_h1[D:D + 1, :, :].bitcast(F32), 1.0).then_inc(consts, 1)
            pool.wait_ge(consts, 4)
            pool.affine_select(out=ident[:, :], in_=ident[:, :], compare_op=ALU.not_equal, fill=1.0,
                               base=0, pattern=[[-1, P]], channel_multiplier=1).then_inc(consts, 1)
            for q in range(P // PER_GROUP):
                g = slice(q * PER_GROUP, (q + 1) * PER_GROUP)
                pool.wait_ge(consts, 5 + q)
                pool.memset(group_avg[g, g], 1.0 / PER_GROUP).then_inc(consts, 1)
            pool.wait_ge(consts, 9)

            def rsqrt():
                nc.gpsimd.tensor_tensor(rstd[:, :], gvar[:, :], minus_half[:, :], ALU.pow).then_inc(rstd_ready, 1)

            for half in range(2):
                start_taken(pool, "var", half)
                rsqrt()

            def lo_part(ring2, r3, count):
                pool.wait_ge(prob_h_ready, count)
                nc.gpsimd.tensor_tensor(prob_l[:, r3, :], prob[:, ring2, :], prob_h[:, r3, :].bitcast(F32),
                                        ALU.subtract).then_inc(prob_l_pool, 1)

            lo_part(1, 1, 2)

            def normalise(s, ahead, tc):
                h = (s.h + ahead) % NH
                r = rows(h)[0]
                if s.section == "body" and s.k == 8:
                    pool.wait_ge(res_bias, s.batches(8, 3 if tc else 6))
                end = s.h == 7 and not s.has_next
                blocks = 0 if s.slots is None else 7 + AHEAD if tc else BLOCKS if end else 15 + AHEAD
                pool.wait_ge(prob_l_pool, s.heads(per_pool, 0, sum(j % BLOCKS in POOL_BLOCKS for j in range(blocks))))
                pool.wait_ge(inv_in, s.heads(32, ahead, 16 * (tc + 1)))
                nc.gpsimd.tensor_tensor(o[r, h // 2, tc * 512:(tc + 1) * 512], acc[r, tc, :], inv_b[r, :],
                                        ALU.mult).then_inc(o_ready, 1)
                pool.wait_ge(o_ready, s.heads(2, ahead, tc + 1))

            def add_bias(s, t):
                pool.wait_ge(res_in[t % RES], tile_count(s, t, 0))
                nc.gpsimd.tensor_tensor(res[:, t % RES, :], res[:, t % RES, :], bias[:, :], ALU.add).then_inc(res_bias, 1)

            def step(s):
                first = s.section == "first"
                end = s.h == 7 and not s.has_next
                for i in range(BLOCKS):
                    ahead, j = divmod(i + AHEAD, BLOCKS)
                    if j in POOL_BLOCKS and not (end and ahead):
                        lo_part(j % 2, ring3(s, i + AHEAD), s.heads(BLOCKS, ahead, j + 1))
                    if i == 6 and not first:
                        normalise(s, -1, 1)
                    if i == 14:
                        normalise(s, 0, 0)
                    if s.has_next and (s.h, i) in ((3, 9), (6, 12)):
                        entry_taken(pool, s, "var", 0 if s.h == 3 else 1)
                        rsqrt()
                    if s.section == "body" and s.k == 8:
                        for t, at in enumerate(PROJ_SLOTS):
                            if i == at:
                                add_bias(s, t)

            pool.wait_ge(bias_in, 16)
            run(pool, step)
            s = Step(pool, B - 1, "last", 8, plan, B, None)
            normalise(s, -1, 1)
            for t in range(TT):
                add_bias(s, t)


_INS = ["x", "L0_conv_Wq", "L0_conv_Wk", "L0_conv_Wv", "L0_conv_Wproj", "L0_conv_bproj"]


def kernel(**inputs):
    import numpy as np
    import concourse.bacc as bacc
    from concourse.bass_utils import run_bass_kernel_spmd

    nc = bacc.Bacc("TRN2", target_bir_lowering=False, num_devices=1)
    arrays, args = {}, []
    for name in _INS:
        a = np.ascontiguousarray(inputs[name])
        arrays[f"in_{name}"] = a
        args.append(nc.dram_tensor(f"in_{name}", a.shape, mybir.dt.from_np(a.dtype), kind="ExternalInput").ap())
    shape = arrays["in_x"].shape
    args.append(nc.dram_tensor("out_x", shape, F32, kind="ExternalOutput").ap())
    attention_block(nc, *args)
    r = run_bass_kernel_spmd(nc, [arrays], core_ids=[0])
    return r.results[0]["out_x"]
```

```python
from contextlib import ExitStack

import concourse.bass as bass
from concourse import mybir

F32 = mybir.dt.float32
F32R = mybir.dt.float32r
ALU = mybir.AluOpType
ACT = mybir.ActivationFunctionType
AX = mybir.AxisListType

P = 128
GROUPS = 32
EPS = 1e-5
ST, SM, PVB, WB = 0, 3, 5, 6

CHUNKS = {"qk": 4, "qn": 4, "v": 4, "xt": 4, "proj": 4, "mean": 1, "var": 1, "mt": 1}
RES = 3
BLOCKS = 16
AHEAD = 3
POOL_BLOCKS = (1, 4, 5, 6, 7, 8, 9, 11, 12, 13, 15)


WORK = {
    "plain": ((1, "mt", 1, 0, 1), (10, "mt", 0, 0, 1), (10, "qn", 0, 0, 3), (12, "qn", 1, 0, 3),
        (12, "qn", 0, 3, 4), (13, "qn", 1, 3, 4)),
    "values": ((1, "mt", 1, 0, 1), (3, "v", 0, 0, 4), (6, "v", 1, 0, 4), (10, "mt", 0, 0, 1),
        (11, "qn", 0, 0, 3), (11, "qn", 1, 0, 2), (12, "qn", 0, 3, 4), (13, "qn", 1, 2, 4)),
    "norm": ((1, "mt", 1, 0, 1), (6, "mean", 0, 0, 1), (9, "var", 0, 0, 1), (10, "mt", 0, 0, 1),
        (11, "qn", 0, 0, 2), (12, "qn", 0, 2, 4), (12, "qn", 1, 0, 2), (13, "qn", 1, 2, 4)),
    "tokens": ((0, "xt", 0, 0, 4), (1, "mt", 1, 0, 1), (2, "xt", 1, 0, 4), (3, "xt", 2, 0, 4),
        (5, "xt", 3, 0, 4), (9, "mean", 1, 0, 1), (10, "mt", 0, 0, 1), (11, "var", 1, 0, 1),
        (14, "xt", 4, 0, 4)),
    "next": ((0, "mt", 1, 0, 1), (1, "xt", 5, 0, 4), (2, "xt", 6, 0, 4), (3, "xt", 7, 0, 4),
        (4, "qk", 0, 0, 4), (5, "qk", 1, 0, 4), (6, "v", 0, 0, 4), (7, "v", 1, 0, 4), (9, "v", 2, 0, 4),
        (10, "v", 3, 0, 4), (11, "mt", 0, 0, 1), (12, "qn", 0, 0, 4), (13, "qn", 1, 0, 4)),
    "proj": ((1, "mt", 1, 0, 1), (3, "proj", 0, 0, 4), (4, "proj", 1, 0, 4), (5, "proj", 2, 0, 4),
        (6, "proj", 3, 0, 4), (8, "proj", 4, 0, 4), (9, "mt", 0, 0, 1), (10, "proj", 5, 0, 4),
        (11, "proj", 6, 0, 4), (12, "qn", 0, 0, 4), (13, "qn", 1, 0, 4), (14, "proj", 7, 0, 4)),
}
MAXIMA = {
    "plain": (0, 0, 2, 1, 1, 1, 2, 0, 1, 2, 1, 2, 1, 1, 1, 0),
    "values": (0, 0, 2, 1, 2, 0, 2, 0, 1, 1, 2, 2, 1, 0, 2, 0),
    "norm": (0, 2, 0, 1, 1, 1, 2, 1, 0, 1, 1, 2, 1, 1, 2, 0),
    "tokens": (0, 1, 1, 1, 1, 1, 1, 1, 1, 2, 1, 2, 1, 2, 0, 0),
    "next": (0, 0, 0, 0, 0, 0, 0, 2, 2, 2, 2, 2, 2, 2, 2, 0),
    "proj": (0, 1, 1, 1, 2, 0, 1, 2, 1, 2, 1, 1, 1, 1, 1, 0),
}
STAT_SLOTS = ((1, 2, 3, 3), (5, 6, 7, 8))
MEAN_SLOTS = (5, 8)
NORM_SLOTS = ((12, 12, 14, 15), (13, 13, 14, 15))
DEN_SLOTS = (9, 1)
INV_SLOTS = (10, 3)
ROWS_SLOTS = (12, 6)
OUT_SLOTS = (15, 7)
FIRST = {
    "plain": ((0, 8), (), (0, 7, 14)),
    "values": ((0, 8), (), ()),
    "norm": ((0, 8), (), ()),
    "tokens": ((0, 8), (15,), (8,)),
    "next": ((0, 8), (), (6, 13, 14)),
    "proj": ((0, 8), (), ()),
}


def step_kind(h, has_next, proj):
    if proj:
        return "proj"
    if h in (1, 2):
        return "values"
    if not has_next:
        return "plain"
    return {3: "norm", 6: "tokens", 7: "next"}.get(h, "plain")


def fillers(h, has_next, proj):
    slots = [[] for _ in range(BLOCKS)]
    for slot, kind, a, lo, hi in WORK[step_kind(h, has_next, proj)]:
        if kind == "v" and h in (1, 2):
            a += 4 + 2 * (h - 1)
        if not has_next and (h >= 6 and kind == "qn" or h == 7 and (kind, a) == ("mt", 0)):
            continue
        slots[slot].append((kind, a, lo, hi))
    return slots


def max_blocks(h, has_next, proj):
    if h == 7 and not has_next:
        return (0,) * BLOCKS
    return MAXIMA[step_kind(h, has_next, proj)]


PROJ_SLOTS = tuple(slot for slot, kind, *_ in WORK["proj"] if kind == "proj")


class Plan:

    def __init__(self, batches):
        self.prologue = [("mean", 0), ("var", 0)] + [("xt", t) for t in range(4)]
        self.prologue += [("mean", 1), ("var", 1)] + [("xt", t) for t in range(4, 8)]
        self.prologue += [("qk", 0), ("qk", 1), ("qn", 0), ("qn", 1), ("v", 0), ("v", 1), ("mt", 0), ("v", 2), ("v", 3)]
        self.place = {("start", 0, e): n for n, e in enumerate(self.prologue)}
        n = len(self.prologue)
        self.steps = {}
        for section, ks in (("first", [0]), ("body", range(1, 9)), ("last", range(1, 8))):
            if section == "last":
                n = body_start + self.per_batch * (batches - 1)
            if section == "body":
                body_start = n
            for k in ks:
                has_next = section != "last"
                slots = fillers(k % 8, has_next, k == 8)
                assert not slots[BLOCKS - 1]
                ends = []
                for s, slot in enumerate(slots):
                    for kind, a, lo, hi in slot:
                        if lo == 0:
                            assert len(ends) < 2 or ends[-2] < s
                            ends.append(BLOCKS)
                        if hi == CHUNKS[kind]:
                            ends[-1] = s
                self.steps[section, k] = slots
                for s in slots:
                    for kind, a, lo, hi in s:
                        if lo == 0:
                            self.place[section, k, (kind, a)] = n
                            n += 1
            if section == "body":
                self.per_batch = n - body_start
        for t in range(8):
            self.place["last", 8, ("proj", t)] = n + t
        assert self.per_batch % 2 == 0


class Step:

    def __init__(self, eng, it, section, k, plan, last_batch, bases):
        self.eng, self.it, self.section, self.k = eng, it, section, k
        self.plan, self.bases = plan, bases
        self.h = k % 8
        self.has_next = section != "last"
        self.slots = plan.steps.get((section, k))
        self.first = FIRST[step_kind(self.h, self.has_next, section == "body" and k == 8)]
        self.looped = section == "body"

    def at(self, per_batch, const):
        if not self.looped:
            return per_batch * self.it + const
        if per_batch not in self.bases:
            self.bases[per_batch] = self.eng.snap(self.it * per_batch)
        return self.bases[per_batch] + const

    def heads(self, per_head, ahead=0, more=0):
        return self.at(8 * per_head, per_head * (self.k + ahead) + more)

    def batches(self, per_batch, more):
        return self.at(per_batch, more)

    def bank(self, kind, arg, back=0):
        n = self.plan.place[self.section, self.k - back, (kind, arg)]
        per = self.plan.per_batch
        if self.looped:
            return n % 2, self.at(per // 2, n // 2)
        return n % 2, n // 2

    def done(self, slot):
        pieces = self.slots[slot - 1] if slot else []
        return [(kind, a) for kind, a, lo, hi in pieces if hi == CHUNKS[kind]]


def attention_block(nc, x, Wq, Wk, Wv, Wproj, bproj, out):
    B, C, H_, W_ = x.shape
    T = H_ * W_
    NH, _, D = Wq.shape
    CH = C // P
    TT = T // P
    TC = T // 512
    SCALE = D ** -0.5
    PER_GROUP = T // GROUPS
    assert (C, T, NH, D, CH, TT, TC) == (512, 1024, 8, 64, 4, 8, 2)
    plan = Plan(B)

    xv = x.rearrange("b c h w -> b (c h w)").rearrange("b (k p c) -> b p k c", p=P, c=C)
    ov = out.rearrange("b c h w -> b (c h w)").rearrange("b (k p c) -> b p k c", p=P, c=C)
    inv_dram = nc.dram_tensor("inv_dram", (1, 512), F32).ap()

    with ExitStack() as ctx:
        def sb(name, shape, dt=F32):
            return ctx.enter_context(nc.sbuf_tensor(name, shape, dt))

        def sem(name):
            return ctx.enter_context(nc.semaphore(name))

        wqk_h = sb("wqk_h", [P, CH, NH, P], F32R)
        wqk_l = sb("wqk_l", [P, CH, NH, P], F32R)
        wv_h = sb("wv_h", [P, CH, C], F32R)
        wv_l = sb("wv_l", [P, CH, C], F32R)
        wp = sb("wp", [P, CH, C])
        bias = sb("bias", [P, C])
        ident = sb("ident", [P, P])
        group_avg = sb("group_avg", [P, P])
        xh = sb("xh", [P, CH, T], F32R)
        xl = sb("xl", [P, CH, T], F32R)
        VW = 2 * D + 1
        vh = sb("vh", [P, TT, NH // 2, VW], F32R)
        vl = sb("vl", [P, TT, NH // 2, VW], F32R)
        q_hh = sb("q_hh", [P, 2, T], F32R)
        q_lm = sb("q_lm", [P, 2, T], F32R)
        k_hl = sb("k_hl", [P, 2, T], F32R)
        k_h1 = sb("k_h1", [P, 2, T], F32R)
        prob = sb("prob", [P, 2, 512])
        prob_h = sb("prob_h", [P, 3, 512], F32R)
        prob_l = sb("prob_l", [P, 3, 512], F32R)
        acc = sb("acc", [P, 2, 512])
        inv_b = sb("inv_b", [P, 512])
        den = sb("den", [32, 16])
        inv = sb("inv", [32, 16])
        o = sb("o", [P, NH // 2, T])
        xs = sb("xs", [P, 4, C])
        res = sb("res", [P, RES, C])
        smax = sb("smax", [P, BLOCKS])
        nmax = sb("nmax", [P, TT])
        mrow = q_lm[96:100, 0, 0:2 * P].rearrange("p (a q) -> p a q", a=2)
        bn = sb("bn", [P, 4, 6])
        mv = sb("mv", [P, 4, 2])
        gmean = sb("gmean", [P, 4])
        dev = sb("dev", [P, 4])
        dev2 = sb("dev2", [P, 4])
        spread = sb("spread", [P, 4])
        gvar = sb("gvar", [P, 4])
        rstd = sb("rstd", [P, 4])
        minus_half = sb("minus_half", [P, 4])

        ps = [ctx.enter_context(nc.psum_tensor(f"bank{n}", [P, 512], F32)) for n in range(8)]

        weights_in = sem("weights_in")
        wv_in = sem("wv_in")
        wp_in = sem("wp_in")
        bias_in = sem("bias_in")
        x_in = [sem(f"x_in{t}") for t in range(4)]
        res_in = [sem(f"res_in{n}") for n in range(RES)]
        y_out = [sem(f"y_out{n}") for n in range(RES)]
        den_in = sem("den_in")
        inv_out = sem("inv_out")
        inv_in = sem("inv_in")
        mrow_in = [sem("mrow_in0"), sem("mrow_in1")]
        w_hi = sem("w_hi")
        w_lo = sem("w_lo")
        consts = sem("consts")
        v_cols = sem("v_cols")
        stat_done = sem("stat_done")
        rstd_ready = sem("rstd_ready")
        xn_ready = sem("xn_ready")
        mean_done = sem("mean_done")
        var_done = sem("var_done")
        xt_done = sem("xt_done")
        qk_done = sem("qk_done")
        v_done = sem("v_done")
        mt_done = sem("mt_done")
        proj_done = sem("proj_done")
        xt_hi = sem("xt_hi")
        qk_hi = sem("qk_hi")
        k_split = sem("k_split")
        qk_twice = [[sem(f"qk_twice{slot}{a}") for a in range(2)] for slot in range(2)]
        v_hi = sem("v_hi")
        taken = [sem("taken0"), sem("taken1")]
        scores_ready = sem("scores_ready")
        rows_ready = sem("rows_ready")
        rows_used = sem("rows_used")
        nmax_ready = sem("nmax_ready")
        prob_h_ready = sem("prob_h_ready")
        prob_l_ready = sem("prob_l_ready")
        prob_l_pool = sem("prob_l_pool")
        pv_done = sem("pv_done")
        acc_ready = sem("acc_ready")
        inv_ready = sem("inv_ready")
        o_ready = sem("o_ready")
        res_bias = sem("res_bias")

        per_pool = len(POOL_BLOCKS)
        per_dve = BLOCKS - per_pool

        def lo_wait(eng, s, i):
            ahead, i = divmod(i, BLOCKS)
            if i in POOL_BLOCKS:
                eng.wait_ge(prob_l_pool, s.heads(per_pool, ahead, POOL_BLOCKS.index(i) + 1))
            else:
                n = sum(j not in POOL_BLOCKS for j in range(i + 1))
                eng.wait_ge(prob_l_ready, s.heads(per_dve, ahead, n))

        def entry_taken(eng, s, kind, a, back=0):
            bank, before = s.bank(kind, a, back)
            eng.wait_ge(taken[bank], before + 1)

        def start_taken(eng, kind, a):
            n = plan.place["start", 0, (kind, a)]
            eng.wait_ge(taken[n % 2], n // 2 + 1)

        def tile_count(s, t, credit=16):
            r = t % RES
            return s.batches(16 * len(range(r, TT, RES)), credit + 16 * (t // RES + 1))

        def rows(h):
            return (slice(0, D), D) if h % 2 == 0 else (slice(D, P), D - 1)

        def run(eng, step):
            step(Step(eng, 0, "first", 0, plan, B, None))
            with eng.Fori(0, B - 1) as it:
                bases = {}
                for k in range(1, 9):
                    step(Step(eng, it, "body", k, plan, B, bases))
            for k in range(1, 8):
                step(Step(eng, B - 1, "last", k, plan, B, None))

        def ring3(s, i):
            return (BLOCKS * s.h + i) % (BLOCKS * NH) % 3

        def early(s, i):
            return int(s.h == 7 and i + AHEAD - BLOCKS in (0, 1))

        block = ctx.enter_context(nc.Block())

        @block.sync
        def _(sp):
            raw_qk = o[:, :, :].rearrange("p a t -> p (a t)").rearrange("p (c h m) -> p c h m", c=CH, h=NH)
            for t in range(4):
                sp.dma_start(xs[:, t, :], xv[0, :, t, :]).then_inc(x_in[t], 16)
            for r in range(RES):
                sp.sem_inc(y_out[r], 16)
            for c in range(CH):
                for half, w in ((0, Wq), (1, Wk)):
                    sp.dma_start(raw_qk[:, c, :, half * D:(half + 1) * D],
                                 w[:, c * P:(c + 1) * P, :].rearrange("h p d -> p h d")).then_inc(weights_in, 16)
            for t in range(4):
                sp.wait_ge(xt_done, t + 1)
                sp.dma_start(xs[:, t, :], xv[0, :, 4 + t, :]).then_inc(x_in[t], 16)
            for c in range(CH):
                sp.dma_start(wp[:, c, :].rearrange("p (h d) -> p h d", h=NH),
                             Wv[:, c * P:(c + 1) * P, :].rearrange("h p d -> p h d")).then_inc(wv_in, 16)
            sp.dma_start(bias[:, :], bproj.partition_broadcast(P)).then_inc(bias_in, 16)
            sp.wait_ge(w_lo, 2)
            sp.dma_start(wp[:, :, :], Wproj.rearrange("(c p) n -> p c n", p=P)).then_inc(wp_in, 16)

            def max_row(half, slot):
                sp.dma_start(q_lm[D:D + 1, slot, half * 512:(half + 1) * 512].bitcast(F32),
                             mrow[:, half, :].bitcast(F32)).then_inc(mrow_in[half], 16)

            def twice(a, slot, count):
                sp.wait_ge(qk_hi, count)
                cols = slice(a * 512, (a + 1) * 512)
                sp.dma_start(q_hh[D:P, slot, cols].bitcast(F32),
                             q_hh[0:D, slot, cols].bitcast(F32)).then_inc(qk_twice[slot][a], 16)
                sp.dma_start(k_hl[0:D, slot, cols].bitcast(F32),
                             k_h1[0:D, slot, cols].bitcast(F32)).then_inc(qk_twice[slot][a], 16)

            twice(0, 0, 1)
            twice(1, 0, 2)
            twice(0, 1, 3)
            twice(1, 1, 4)
            start_taken(sp, "mt", 0)
            max_row(0, 0)

            def den_to_square(s, ahead, tc):
                sp.wait_ge(acc_ready, s.heads(2, ahead, tc + 1))
                r = rows(s.h + ahead)[1]
                sp.dma_start(den[:, :], acc[r:r + 1, tc, :]).then_inc(den_in, 16)

            def inv_to_rows(s, ahead, tc):
                sp.wait_ge(inv_ready, s.heads(2, ahead, tc + 1))
                sp.dma_start(inv_dram[0:1, :].rearrange("a (p f) -> (a p) f", p=32), inv[:, :]).then_inc(inv_out, 16)
                sp.wait_ge(inv_out, s.heads(32, ahead, 16 * (tc + 1)))
                sp.dma_start(inv_b[rows(s.h + ahead)[0], :],
                             inv_dram[0, :].partition_broadcast(D)).then_inc(inv_in, 16)

            def residual(s, t, b):
                sp.wait_ge(y_out[t % RES], tile_count(s, t - RES))
                sp.dma_start(res[:, t % RES, :], xv[b, :, t, :]).then_inc(res_in[t % RES], 16)

            def store(s, t, b):
                entry_taken(sp, s, "proj", t)
                sp.dma_start(ov[b, :, t, :], res[:, t % RES, :]).then_inc(y_out[t % RES], 16)

            def step(s):
                first = s.section == "first"
                for i in range(BLOCKS):
                    if i == DEN_SLOTS[1] and not first:
                        den_to_square(s, -1, 1)
                    for kind, a in s.done(i):
                        if kind == "qk":
                            twice(a, (s.k + 1) % 2, s.heads(2, 1, a + 1))
                        if kind == "mt":
                            entry_taken(sp, s, "mt", a)
                            max_row(a, (s.k + 1 - a) % 2)
                        if kind == "qn":
                            twice(a, s.k % 2, s.heads(2, 2, a + 1))
                    if i == ROWS_SLOTS[1] and not first:
                        inv_to_rows(s, -1, 1)
                    if i == DEN_SLOTS[0]:
                        den_to_square(s, 0, 0)
                    if i == ROWS_SLOTS[0]:
                        inv_to_rows(s, 0, 0)
                    if s.h == 2 and i == 8 and s.has_next:
                        sp.wait_ge(xt_done, s.batches(8, 8))
                        for t in range(4):
                            sp.dma_start(xs[:, t, :], xv[s.it + 1, :, t, :]).then_inc(x_in[t], 16)
                    for kind, a in s.done(i):
                        if kind == "xt" and a < 4:
                            sp.wait_ge(xt_done, s.batches(8, 8 + a + 1))
                            sp.dma_start(xs[:, a, :], xv[s.it + 1, :, 4 + a, :]).then_inc(x_in[a], 16)
                    if s.section == "body" and s.k == 8:
                        if i < RES:
                            residual(s, i, s.it)
                        for t, at in enumerate(PROJ_SLOTS):
                            if i == at + 1:
                                store(s, t, s.it)
                                if 1 <= t <= TT - RES:
                                    residual(s, t + RES - 1, s.it)

            run(sp, step)
            s = Step(sp, B - 1, "last", 8, plan, B, None)
            den_to_square(s, -1, 1)
            for t in range(RES):
                residual(s, t, B - 1)
            inv_to_rows(s, -1, 1)
            for t in range(TT):
                store(s, t, B - 1)
                if 1 <= t <= TT - RES:
                    residual(s, t + RES - 1, B - 1)
            for t in range(TT - RES, TT):
                sp.wait_ge(y_out[t % RES], tile_count(s, t))

        @block.tensor
        def _(pe):
            def split_product(bank, cols, pairs, start, stop):
                n = len(pairs)
                for j, (w, m) in enumerate(pairs):
                    last = nc.tensor.matmul(ps[bank][:, cols], w, m, start=start and j == 0,
                                            stop=stop and j == n - 1)
                return last

            def entry(kind, a, lo, hi, bank, before, head, wait):
                w = ps[WB + bank]
                if lo == 0 and before is not None:
                    pe.wait_ge(taken[bank], before)
                wait()
                if kind in ("qk", "qn"):
                    cols = slice(a * 512, (a + 1) * 512)
                    for c in range(lo, hi):
                        last = split_product(WB + bank, slice(0, 512),
                                             [(wqk_h[:, c, head, :], xh[:, c, cols]),
                                              (wqk_l[:, c, head, :], xh[:, c, cols]),
                                              (wqk_h[:, c, head, :], xl[:, c, cols])], c == 0, c == CH - 1)
                    if hi == CH:
                        last.then_inc(qk_done, 1)
                elif kind == "v":
                    half, e = divmod(a, 4)
                    vcols = slice(half * 256, (half + 1) * 256)
                    for j in range(2):
                        t = slice((2 * e + j) * P, (2 * e + j + 1) * P)
                        for c in range(CH):
                            last = split_product(WB + bank, slice(j * 256, (j + 1) * 256),
                                                 [(xh[:, c, t], wv_h[:, c, vcols]),
                                                  (xh[:, c, t], wv_l[:, c, vcols]),
                                                  (xl[:, c, t], wv_h[:, c, vcols])], c == 0, c == CH - 1)
                    last.then_inc(v_done, 1)
                elif kind == "xt":
                    for c in range(CH):
                        last = nc.tensor.transpose(w[:, c * P:(c + 1) * P], xs[:, a % 4, c * P:(c + 1) * P],
                                                   ident[:, :])
                    last.then_inc(xt_done, 1)
                elif kind == "mean":
                    nc.tensor.matmul(w[:, 0:4], group_avg[:, :], mv[:, :, 0], start=True, stop=True).then_inc(mean_done, 1)
                elif kind == "var":
                    nc.tensor.matmul(w[:, 0:4], group_avg[:, :], spread[:, :], start=True, stop=True).then_inc(var_done, 1)
                elif kind == "mt":
                    nc.tensor.matmul(w[0:4, 0:P], nmax[:, a * 4:(a + 1) * 4], ident[:, :],
                                     start=True, stop=True).then_inc(mt_done, 1)
                elif kind == "proj":
                    for c in range(CH):
                        last = nc.tensor.matmul(w[:, :], o[:, c, a * P:(a + 1) * P], wp[:, c, :],
                                                start=c == 0, stop=c == CH - 1)
                    last.then_inc(proj_done, 1)

            def scores(slot, i, n_bank, wait):
                tc, t = divmod(i, TT)
                keys, queries = slice(t * P, (t + 1) * P), slice(tc * 512, (tc + 1) * 512)
                wait()
                s_bank = ps[ST + n_bank]
                nc.tensor.matmul(s_bank[:, :], k_hl[:, slot, keys], q_hh[:, slot, queries], start=True, stop=False)
                nc.tensor.matmul(s_bank[:, :], k_h1[0:D + 1, slot, keys], q_lm[0:D + 1, slot, queries],
                                 start=False, stop=True).then_inc(scores_ready, 1)

            def row_scores(slot, j):
                t, half = divmod(j, 2)
                nc.tensor.matmul(ps[SM + j % 2][:, :], q_hh[:, slot, t * P:(t + 1) * P],
                                 k_hl[:, slot, half * 512:(half + 1) * 512], start=True, stop=True).then_inc(rows_ready, 1)

            nothing = lambda: None
            n = 0

            def start_entry(kind, a, h=0, wait=nothing):
                pos = plan.place["start", 0, (kind, a)]
                before = pos // 2 if pos >= 2 else None
                entry(kind, a, 0, 4 if kind in ("qk", "qn", "v", "xt") else 1, pos % 2, before, h, wait)

            pe.wait_ge(consts, 9)
            for half in range(2):
                start_entry("mean", half, wait=lambda: pe.wait_ge(stat_done, 11 * half + 8))
                start_entry("var", half, wait=lambda: start_taken(pe, "mean", half))
                for t in range(4 * half, 4 * half + 4):
                    start_entry("xt", t, wait=lambda: pe.wait_ge(xn_ready, t + 1))
            pe.wait_ge(w_hi, 1)
            pe.wait_ge(w_lo, 1)
            for tc in range(2):
                for t in range(4 * tc + 2, 4 * tc + 4):
                    start_taken(pe, "xt", t)
                start_entry("qk", tc)
            for tc in range(2):
                start_entry("qn", tc, 1)
            pe.wait_ge(w_hi, 2)
            pe.wait_ge(w_lo, 2)
            start_entry("v", 0)
            start_entry("v", 1)
            for tc in range(2):
                start_taken(pe, "qk", tc)
                pe.wait_ge(qk_twice[0][tc], 32)
            for j in range(BLOCKS):
                if j >= 2:
                    pe.wait_ge(rows_used, j - 1)
                row_scores(0, j)
                if j == 9:
                    start_entry("mt", 0, wait=lambda: pe.wait_ge(nmax_ready, 1))
            start_entry("v", 2)
            start_entry("v", 3)
            scores(0, 0, 0, lambda: pe.wait_ge(mrow_in[0], 16))
            scores(0, 1, 1, nothing)
            scores(0, 2, 2, nothing)
            pe.wait_ge(v_cols, 2)
            pe.wait_ge(wp_in, 16)

            def other_work(s, i):
                for kind, a, lo, hi in s.slots[i]:
                    bk, before = s.bank(kind, a)

                    def wait():
                        if kind == "xt":
                            pe.wait_ge(xn_ready, s.batches(8, 8 + a + 1))
                        if kind == "mean":
                            pe.wait_ge(stat_done, s.batches(22, 22 + 11 * a + 8))
                        if kind == "var":
                            entry_taken(pe, s, "mean", a)
                        if kind == "mt":
                            pe.wait_ge(nmax_ready, s.heads(2, 0 if a else 1, 2 if a else 1))
                        if kind == "proj" and a in (0, 4):
                            pe.wait_ge(o_ready, s.heads(2, 0, -1 if a == 0 else 0))
                    entry(kind, a, lo, hi, bk, before, (s.h + (2 if kind == "qn" else 1)) % NH, wait)
                per_slot = max_blocks(s.h, s.has_next, s.section == "body" and s.k == 8)
                for j in range(sum(per_slot[:i]), sum(per_slot[:i + 1])):
                    if j == 0:
                        pe.wait_ge(k_split, s.heads(2, 1, 2))
                        for a in range(2):
                            pe.wait_ge(qk_twice[(s.k + 1) % 2][a], s.at(16 * NH, 32 * ((s.k + 1) // 2 + 1)))
                    pe.wait_ge(rows_used, s.heads(BLOCKS, 1, j - 1))
                    row_scores((s.k + 1) % 2, j)

            def step(s):
                first = s.section == "first"
                end = s.h == 7 and not s.has_next
                for i in range(BLOCKS):
                    ahead, j = divmod(i + AHEAD, BLOCKS)
                    if not (end and ahead):
                        def wait():
                            pe.wait_ge(prob_h_ready, s.heads(BLOCKS, 0, i + 1 + early(s, i)))
                            if j == 0:
                                pe.wait_ge(mrow_in[0], s.heads(16, 1, 16))
                            if j == TT:
                                pe.wait_ge(mrow_in[1], s.heads(16, 0, 16))
                        scores((s.k + ahead) % 2, j, ring3(s, i + AHEAD), wait)
                    if i in s.first[0]:
                        other_work(s, i)
                    tc, t = divmod(i, TT)
                    pair = s.h // 2
                    if t == 0 and not (first and tc == 0):
                        pe.wait_ge(acc_ready, s.heads(2, 0, tc))
                    if tc == 0 and t % 2 == 0 and s.h in (0, 4):
                        if first:
                            start_taken(pe, "v", t // 2)
                        elif s.h == 0:
                            entry_taken(pe, s, "v", t // 2, back=1)
                        else:
                            entry_taken(pe, s, "v", 4 + t // 2, back=3 - t // 4)
                    lo_wait(pe, s, i)
                    ring = ring3(s, i)
                    c0 = 0 if s.h % 2 == 0 else 1
                    v_hi_op, v_lo_op = vh[:, t, pair, c0:c0 + P], vl[:, t, pair, c0:c0 + P]
                    bank = PVB
                    nc.tensor.matmul(ps[bank][:, :], v_hi_op, prob_h[:, ring, :], start=t == 0, stop=False)
                    nc.tensor.matmul(ps[bank][:, :], v_lo_op, prob_h[:, ring, :], start=False, stop=False)
                    nc.tensor.matmul(ps[bank][:, :], v_hi_op, prob_l[:, ring, :],
                                     start=False, stop=t == TT - 1).then_inc(pv_done, 1)
                    if i not in s.first[0]:
                        other_work(s, i)

            run(pe, step)
            s = Step(pe, B - 1, "last", 8, plan, B, None)
            pe.wait_ge(o_ready, 2 * NH * B)
            for t in range(TT):
                bk, before = s.bank("proj", t)
                entry("proj", t, 0, 4, bk, before, 0, nothing)

        @block.scalar
        def _(act):
            raw_qk = o[:, :, :].rearrange("p a t -> p (a t)").rearrange("p (c h m) -> p c h m", c=CH, h=NH)

            def exp_to(out, bank):
                return nc.scalar.activation(out, ps[ST + bank][:, :], ACT.Exp, scale=SCALE)

            def take(kind, a, bank, slot, count):
                w = ps[WB + bank]
                if kind == "xt":
                    act.wait_ge(xt_done, count)
                    nc.scalar.copy(xh[:, :, a * P:(a + 1) * P],
                                   w[:, :].rearrange("p (c t) -> p c t", c=CH)).then_inc(xt_hi, 1)
                if kind in ("qk", "qn"):
                    cols = slice(a * 512, (a + 1) * 512)
                    act.wait_ge(qk_done, count)
                    nc.scalar.copy(q_hh[0:D, slot, cols], w[0:D, :])
                    nc.scalar.copy(k_h1[0:D, slot, cols], w[D:P, :]).then_inc(qk_hi, 1)
                if kind == "v":
                    half, e = divmod(a, 4)
                    act.wait_ge(v_done, count)
                    for j in range(2):
                        for odd in range(2):
                            last = nc.scalar.copy(
                                vh[:, 2 * e + j, 2 * half:2 * half + 2, odd * (D + 1):odd * (D + 1) + D],
                                w[:, j * 256:(j + 1) * 256].rearrange("p (a o d) -> p o a d", o=2, d=D)[:, odd])
                    last.then_inc(v_hi, 1)

            act.wait_ge(v_cols, 2)
            for kind, a in plan.prologue:
                if (kind, a) == ("xt", 4):
                    act.wait_ge(weights_in, 128)
                    nc.scalar.copy(wqk_h[:, :, :, :], raw_qk).then_inc(w_hi, 1)
                if (kind, a) == ("qk", 0):
                    act.wait_ge(wv_in, 64)
                    nc.scalar.copy(wv_h[:, :, :], wp[:, :, :]).then_inc(w_hi, 1)
                if kind in ("xt", "qk", "qn", "v"):
                    qn = kind == "qn"
                    take(kind, a, plan.place["start", 0, (kind, a)] % 2, int(qn), a + (3 if qn else 1))
            for n in range(AHEAD):
                act.wait_ge(scores_ready, n + 1)
                if n == 2:
                    act.wait_ge(prob_l_ready, 1)
                exp_to(prob[:, n % 2, :], n)
                exp_to(prob_h[:, n, :], n).then_inc(prob_h_ready, 1)

            def step(s):
                first = s.section == "first"
                end = s.h == 7 and not s.has_next
                for i in range(BLOCKS):
                    ahead, j = divmod(i + AHEAD, BLOCKS)
                    late = i in s.first[2]
                    if late:
                        for kind, a in s.done(i):
                            take_in_step(s, kind, a)
                    if not (end and ahead):
                        r3 = ring3(s, i + AHEAD)
                        act.wait_ge(scores_ready, s.heads(BLOCKS, ahead, j + 1))
                        lo_wait(act, s, i + 1)
                        exp_to(prob[:, j % 2, :], r3)
                    if i % TT == TT - 1:
                        copy_out(s, i // TT)
                    if not (end and ahead):
                        act.wait_ge(pv_done, s.heads(BLOCKS, 0, i + 1 + early(s, i)))
                        exp_to(prob_h[:, r3, :], r3).then_inc(prob_h_ready, 1)
                    if not late:
                        for kind, a in s.done(i):
                            take_in_step(s, kind, a)

            def copy_out(s, tc):
                act.wait_ge(pv_done, s.heads(BLOCKS, 0, 8 * (tc + 1)))
                if s.section != "first":
                    act.wait_ge(o_ready, s.heads(2, 0, tc - 1))
                nc.scalar.copy(acc[:, tc, :], ps[PVB][:, :]).then_inc(acc_ready, 1)

            def take_in_step(s, kind, a):
                bk, _ = s.bank(kind, a) if kind in ("xt", "qk", "qn", "v") else (0, 0)
                if kind == "qk":
                    take(kind, a, bk, (s.k + 1) % 2, s.heads(2, 1, a + 1))
                if kind == "qn":
                    take(kind, a, bk, s.k % 2, s.heads(2, 2, a + 1))
                if kind == "v":
                    take(kind, a, bk, 0, s.batches(8, (8 if s.h == 7 else 0) + a + 1))
                if kind == "xt":
                    take(kind, a, bk, 0, s.batches(8, 8 + a + 1))

            run(act, step)

        @block.vector
        def _(dve):
            raw_qk = o[:, :, :].rearrange("p a t -> p (a t)").rearrange("p (c h m) -> p c h m", c=CH, h=NH)

            def lo_part(ring2, r3, wait):
                wait()
                nc.vector.tensor_tensor(prob_l[:, r3, :], prob[:, ring2, :], prob_h[:, r3, :].bitcast(F32),
                                        ALU.subtract).then_inc(prob_l_ready, 1)

            def token_stats(t, x_count):
                dve.wait_ge(x_in[t], x_count)
                nc.vector.bn_stats(bn[:, t, :], xs[:, t, :]).then_inc(stat_done, 1)

            def token_mean():
                for t in range(4):
                    nc.vector.bn_aggr(mv[:, t, :], bn[:, t, :]).then_inc(stat_done, 1)

            def take_mean(bank, count, at):
                w = ps[WB + bank]
                dve.wait_ge(mean_done, count)
                nc.vector.tensor_copy(gmean[:, :], w[:, 0:4]).then_inc(stat_done, 1)
                nc.vector.tensor_tensor(dev[:, :], mv[:, :, 0], w[:, 0:4], ALU.subtract).then_inc(stat_done, 1)
                dve.wait_ge(stat_done, at(10))
                nc.vector.tensor_tensor(dev2[:, :], dev[:, :], dev[:, :], ALU.mult).then_inc(stat_done, 1)
                dve.wait_ge(stat_done, at(11))
                nc.vector.tensor_tensor(spread[:, :], dev2[:, :], mv[:, :, 1], ALU.add).then_inc(taken[bank], 1)

            def take_var(bank, count):
                dve.wait_ge(var_done, count)
                nc.vector.tensor_scalar(gvar[:, :], ps[WB + bank][:, 0:4], EPS, None, ALU.add).then_inc(taken[bank], 1)

            def norm(t, count):
                dve.wait_ge(rstd_ready, count)
                nc.vector.tensor_scalar(xs[:, t, :], xs[:, t, :], gmean[:, t:t + 1], rstd[:, t:t + 1],
                                        ALU.subtract, ALU.mult).then_inc(xn_ready, 1)

            def take(kind, a, bank, slot, count, hi_count):
                w = ps[WB + bank]
                if kind == "xt":
                    dve.wait_ge(xt_hi, count)
                    cols = slice(a * P, (a + 1) * P)
                    nc.vector.tensor_tensor(xl[:, :, cols], w[:, :].rearrange("p (c t) -> p c t", c=CH),
                                            xh[:, :, cols].bitcast(F32), ALU.subtract).then_inc(taken[bank], 1)
                if kind in ("qk", "qn"):
                    cols = slice(a * 512, (a + 1) * 512)
                    dve.wait_ge(qk_hi, hi_count)
                    nc.vector.tensor_tensor(k_hl[D:P, slot, cols], w[D:P, :], k_h1[0:D, slot, cols].bitcast(F32),
                                            ALU.subtract).then_inc(k_split, 1)
                    nc.vector.tensor_tensor(q_lm[0:D, slot, cols], w[0:D, :], q_hh[0:D, slot, cols].bitcast(F32),
                                            ALU.subtract).then_inc(taken[bank], 1)
                if kind == "v":
                    half, e = divmod(a, 4)
                    dve.wait_ge(v_hi, count)
                    for j in range(2):
                        for odd in range(2):
                            at = (slice(None), 2 * e + j, slice(2 * half, 2 * half + 2),
                                  slice(odd * (D + 1), odd * (D + 1) + D))
                            last = nc.vector.tensor_tensor(
                                vl[at], w[:, j * 256:(j + 1) * 256].rearrange("p (a o d) -> p o a d", o=2, d=D)[:, odd],
                                vh[at].bitcast(F32), ALU.subtract)
                    last.then_inc(taken[bank], 1)

            def take_max(j, count):
                dve.wait_ge(rows_ready, count)
                nc.vector.tensor_reduce(smax[:, j:j + 1], ps[SM + j % 2][:, :], AX.X, ALU.max).then_inc(rows_used, 1)

            def combine(half, used):
                dve.wait_ge(rows_used, used)
                nc.vector.tensor_reduce(nmax[:, 4 * half:4 * half + 4],
                                        smax[:, 8 * half:8 * half + 8].rearrange("p (t a) -> p t a", a=2),
                                        AX.X, ALU.max, negate=True).then_inc(nmax_ready, 1)

            def take_rows(half, bank, count):
                dve.wait_ge(mt_done, count)
                nc.vector.tensor_copy(mrow[:, half, :], ps[WB + bank][0:4, 0:P]).then_inc(taken[bank], 1)

            for tensor, value in ((vh, 1.0), (vl, 0.0)):
                nc.vector.memset(tensor[:, :, :, D:D + 1].bitcast(F32), value).then_inc(v_cols, 1)
            for t in range(4):
                token_stats(t, 16)
            dve.wait_ge(stat_done, 4)
            token_mean()
            for kind, a in plan.prologue:
                bk = plan.place["start", 0, (kind, a)] % 2
                if (kind, a) == ("xt", 5):
                    dve.wait_ge(w_hi, 1)
                    nc.vector.tensor_tensor(wqk_l[:, :, :, :].rearrange("p c h m -> p (c h m)"),
                                            o[:, :, :].rearrange("p a t -> p (a t)"),
                                            wqk_h[:, :, :, :].rearrange("p c h m -> p (c h m)").bitcast(F32),
                                            ALU.subtract).then_inc(w_lo, 1)
                if (kind, a) == ("qk", 0):
                    dve.wait_ge(w_hi, 2)
                    nc.vector.tensor_tensor(wv_l[:, :, :], wp[:, :, :], wv_h[:, :, :].bitcast(F32),
                                            ALU.subtract).then_inc(w_lo, 1)
                if kind == "mean":
                    if a:
                        for t in range(4):
                            token_stats(t, 32)
                        dve.wait_ge(stat_done, 15)
                        token_mean()
                    take_mean(bk, a + 1, lambda n: 11 * a + n)
                elif kind == "var":
                    take_var(bk, a + 1)
                    for t in range(4):
                        norm(t, a + 1)
                elif kind == "mt":
                    take_rows(0, bk, 1)
                    for j in range(10, BLOCKS):
                        take_max(j, j + 1)
                    combine(1, BLOCKS)
                else:
                    qn = kind == "qn"
                    take(kind, a, bk, int(qn), a + 1, a + (3 if qn else 1))
                if (kind, a) == ("v", 1):
                    for j in range(10):
                        take_max(j, j + 1)
                        if j == 7:
                            combine(0, 8)
            for n in range(AHEAD):
                if n in POOL_BLOCKS:
                    continue
                lo_part(n % 2, n, lambda: dve.wait_ge(prob_h_ready, n + 1))

            def step(s):
                first = s.section == "first"
                end = s.h == 7 and not s.has_next
                per_slot = max_blocks(s.h, s.has_next, s.section == "body" and s.k == 8)
                hj = 0
                for i in range(BLOCKS):
                    ahead, j = divmod(i + AHEAD, BLOCKS)
                    if s.h in (3, 6) and s.has_next:
                        half = int(s.h == 6)
                        for t in range(4):
                            if STAT_SLOTS[half][t] == i:
                                token_stats(t, s.batches(32, 48 + 16 * half))
                    token_means = s.has_next and (s.h, i) in ((3, MEAN_SLOTS[0]), (6, MEAN_SLOTS[1]))
                    if token_means:
                        dve.wait_ge(stat_done, s.batches(22, 22 + 11 * (s.h == 6) + 4))
                    for kind, a in s.done(i):
                        if kind == "mt":
                            take_rows(a, s.bank(kind, a)[0], s.heads(2, 0 if a else 1, 2 if a else 1))
                    def maxima():
                        nonlocal hj
                        for _ in range(per_slot[i - 1] if i else 0):
                            take_max(hj, s.heads(BLOCKS, 1, hj + 1))
                            hj += 1
                            if hj in (8, 16):
                                combine(hj // 8 - 1, s.heads(BLOCKS, 1, hj))
                    if i not in s.first[1]:
                        maxima()
                    if s.h == 7 and i == 14 and not end:
                        lo_part(0, ring3(s, 13 + AHEAD), lambda: dve.wait_ge(prob_h_ready, s.heads(BLOCKS, 1, 1)))
                    if j not in POOL_BLOCKS and not (end and ahead) and not (s.h == 7 and i == 13):
                        lo_part(j % 2, ring3(s, i + AHEAD),
                                lambda: dve.wait_ge(prob_h_ready, s.heads(BLOCKS, ahead, j + 1)))
                    if i in s.first[1]:
                        maxima()
                    if token_means:
                        token_mean()
                    for kind, a in s.done(i):
                        bk, _ = s.bank(kind, a)
                        if kind == "qk":
                            take(kind, a, bk, (s.k + 1) % 2, None, s.heads(2, 1, a + 1))
                        elif kind == "qn":
                            take(kind, a, bk, s.k % 2, None, s.heads(2, 2, a + 1))
                        elif kind == "v":
                            take(kind, a, bk, 0, s.batches(8, (8 if s.h == 7 else 0) + a + 1), None)
                        elif kind == "xt":
                            take(kind, a, bk, 0, s.batches(8, 8 + a + 1), None)
                        elif kind == "mean":
                            take_mean(bk, s.batches(2, 2 + a + 1), lambda n: s.batches(22, 22 + 11 * a + n))
                        elif kind == "var":
                            take_var(bk, s.batches(2, 2 + a + 1))
                        elif kind == "proj":
                            output(s, a, bk)
                    if i == INV_SLOTS[1] and not first:
                        reciprocal(s, -1, 1)
                    if i == INV_SLOTS[0]:
                        reciprocal(s, 0, 0)
                    if s.h in (3, 6) and s.has_next:
                        half = int(s.h == 6)
                        for t in range(4):
                            if NORM_SLOTS[half][t] == i:
                                norm(t, s.batches(2, 2 + half + 1))

            def reciprocal(s, ahead, tc):
                if not (s.section == "first" and tc == 0):
                    dve.wait_ge(o_ready, s.heads(2, ahead, tc))
                dve.wait_ge(den_in, s.heads(32, ahead, 16 * (tc + 1)))
                nc.vector.reciprocal(inv[:, :], den[:, :]).then_inc(inv_ready, 1)

            def output(s, t, bank):
                dve.wait_ge(proj_done, s.batches(8, t + 1))
                dve.wait_ge(res_bias, s.batches(8, t + 1))
                nc.vector.tensor_tensor(res[:, t % RES, :], ps[WB + bank][:, :], res[:, t % RES, :], ALU.add).then_inc(taken[bank], 1)

            run(dve, step)
            s = Step(dve, B - 1, "last", 8, plan, B, None)
            reciprocal(s, -1, 1)
            for t in range(TT):
                output(s, t, s.bank("proj", t)[0])

        @block.gpsimd
        def _(pool):
            pool.memset(ident[:, :], 0.0).then_inc(consts, 1)
            pool.memset(group_avg[:, :], 0.0).then_inc(consts, 1)
            pool.memset(minus_half[:, :], -0.5).then_inc(consts, 1)
            pool.wait_ge(consts, 3)
            pool.memset(k_h1[D:D + 1, :, :].bitcast(F32), 1.0).then_inc(consts, 1)
            pool.wait_ge(consts, 4)
            pool.affine_select(out=ident[:, :], in_=ident[:, :], compare_op=ALU.not_equal, fill=1.0,
                               base=0, pattern=[[-1, P]], channel_multiplier=1).then_inc(consts, 1)
            for q in range(P // PER_GROUP):
                g = slice(q * PER_GROUP, (q + 1) * PER_GROUP)
                pool.wait_ge(consts, 5 + q)
                pool.memset(group_avg[g, g], 1.0 / PER_GROUP).then_inc(consts, 1)
            pool.wait_ge(consts, 9)

            def rsqrt():
                nc.gpsimd.tensor_tensor(rstd[:, :], gvar[:, :], minus_half[:, :], ALU.pow).then_inc(rstd_ready, 1)

            for half in range(2):
                start_taken(pool, "var", half)
                rsqrt()

            def lo_part(ring2, r3, count):
                pool.wait_ge(prob_h_ready, count)
                nc.gpsimd.tensor_tensor(prob_l[:, r3, :], prob[:, ring2, :], prob_h[:, r3, :].bitcast(F32),
                                        ALU.subtract).then_inc(prob_l_pool, 1)

            lo_part(1, 1, 2)

            def normalise(s, ahead, tc):
                h = (s.h + ahead) % NH
                r = rows(h)[0]
                if s.section == "body" and s.k == 8:
                    pool.wait_ge(res_bias, s.batches(8, sum(p < OUT_SLOTS[tc] for p in PROJ_SLOTS)))
                end = s.h == 7 and not s.has_next
                blocks = 0 if s.slots is None else min(OUT_SLOTS[tc] + 1 + AHEAD, BLOCKS if end else 99)
                pool.wait_ge(prob_l_pool, s.heads(per_pool, 0, sum(j % BLOCKS in POOL_BLOCKS for j in range(blocks))))
                pool.wait_ge(inv_in, s.heads(32, ahead, 16 * (tc + 1)))
                nc.gpsimd.tensor_tensor(o[r, h // 2, tc * 512:(tc + 1) * 512], acc[r, tc, :], inv_b[r, :],
                                        ALU.mult).then_inc(o_ready, 1)
                pool.wait_ge(o_ready, s.heads(2, ahead, tc + 1))

            def add_bias(s, t):
                pool.wait_ge(res_in[t % RES], tile_count(s, t, 0))
                nc.gpsimd.tensor_tensor(res[:, t % RES, :], res[:, t % RES, :], bias[:, :], ALU.add).then_inc(res_bias, 1)

            def step(s):
                first = s.section == "first"
                end = s.h == 7 and not s.has_next
                for i in range(BLOCKS):
                    ahead, j = divmod(i + AHEAD, BLOCKS)
                    if j in POOL_BLOCKS and not (end and ahead):
                        lo_part(j % 2, ring3(s, i + AHEAD), s.heads(BLOCKS, ahead, j + 1))
                    if i == OUT_SLOTS[1] and not first:
                        normalise(s, -1, 1)
                    if i == OUT_SLOTS[0]:
                        normalise(s, 0, 0)
                    if any(kind == "var" for kind, a in s.done(i)):
                        entry_taken(pool, s, "var", 0 if s.h == 3 else 1)
                        rsqrt()
                    if s.section == "body" and s.k == 8:
                        for t, at in enumerate(PROJ_SLOTS):
                            if i == at:
                                add_bias(s, t)

            pool.wait_ge(bias_in, 16)
            run(pool, step)
            s = Step(pool, B - 1, "last", 8, plan, B, None)
            normalise(s, -1, 1)
            for t in range(TT):
                add_bias(s, t)


_INS = ["x", "L0_conv_Wq", "L0_conv_Wk", "L0_conv_Wv", "L0_conv_Wproj", "L0_conv_bproj"]


def kernel(**inputs):
    import numpy as np
    import concourse.bacc as bacc
    from concourse.bass_utils import run_bass_kernel_spmd

    nc = bacc.Bacc("TRN2", target_bir_lowering=False, num_devices=1)
    arrays, args = {}, []
    for name in _INS:
        a = np.ascontiguousarray(inputs[name])
        arrays[f"in_{name}"] = a
        args.append(nc.dram_tensor(f"in_{name}", a.shape, mybir.dt.from_np(a.dtype), kind="ExternalInput").ap())
    shape = arrays["in_x"].shape
    args.append(nc.dram_tensor("out_x", shape, F32, kind="ExternalOutput").ap())
    attention_block(nc, *args)
    r = run_bass_kernel_spmd(nc, [arrays], core_ids=[0])
    return r.results[0]["out_x"]
```
